# Optimizing a Trainium2 kernel written in Bass

```python
import numpy as np
import jax
import jax.numpy as jnp

def _softmax(x, axis=-1):
    return jax.nn.softmax(x, axis=axis)

def _gelu(x):
    return jax.nn.gelu(x, approximate=True)

def _silu(x):
    return jax.nn.silu(x)

def _sigmoid(x):
    return jax.nn.sigmoid(x)

def _layernorm(x, axis=-1, eps=1e-05):
    m = jnp.mean(x, axis=axis, keepdims=True)
    v = jnp.var(x, axis=axis, keepdims=True)
    return (x - m) / jnp.sqrt(v + eps)

def _scatter_add(tgt, idx, src, axis=0):
    return tgt.at[idx].add(src)

def _segment_sum(src, seg, n):
    return jax.ops.segment_sum(src, seg, n)
kernel_name = 'mk_gnn_resnorm_d2_gnn_r64_092025'

def setup_inputs(seed: int=0):
    np.random.seed(seed)
    _w = jnp.asarray

    def _rec_inputs():
        import jax
        import jax.numpy as jnp
        _gk = jax.random.key(seed)
        x = -0.0003713 + 1 * jax.random.normal(jax.random.fold_in(_gk, 1), (50000, 256), jnp.float32)
        src = jax.random.randint(jax.random.fold_in(_gk, 2), (12500,), 0, 50000, jnp.int32)
        dst = jnp.minimum((50000 * jax.random.uniform(jax.random.fold_in(_gk, 3), (12500,)) ** 2.0).astype(jnp.int32), 49999)
        _o = jnp.argsort(dst, stable=True)
        src = src[_o]
        dst = dst[_o]
        return (x, src, dst)
    x, src, dst = _rec_inputs()

    def _L0_gnn_setup():
        import jax, jax.numpy as jnp
        import numpy as np
        N_NODES = 50000
        N_EDGES = 25000
        H_SIZE = 256
        HEADS = 8
        HEAD_DIM = H_SIZE // HEADS
        NEG_SLOPE = 0.2
        key = jax.random.key(seed)
        k_x, k_e, k_w, k_as, k_ad, k_b = jax.random.split(key, 6)
        x = jax.random.normal(k_x, (N_NODES, H_SIZE), dtype=jnp.float32)
        edge_index = jax.random.randint(k_e, (2, N_EDGES), 0, N_NODES, dtype=jnp.int64)
        scale = 1.0 / np.sqrt(H_SIZE)
        W = jax.random.normal(k_w, (H_SIZE, HEADS, HEAD_DIM), dtype=jnp.float32) * scale
        att_src = jax.random.normal(k_as, (HEADS, HEAD_DIM), dtype=jnp.float32) * scale
        att_dst = jax.random.normal(k_ad, (HEADS, HEAD_DIM), dtype=jnp.float32) * scale
        bias = jnp.zeros((H_SIZE,), dtype=jnp.float32)
        return {'x': x, 'edge_index': edge_index, 'W': W, 'att_src': att_src, 'att_dst': att_dst, 'bias': bias}
    _L0_gnn_all = _L0_gnn_setup()
    _L0_gnn_in = {k: v for k, v in _L0_gnn_all.items() if k in ('W', 'att_src', 'att_dst', 'bias')}
    del _L0_gnn_all

    def _L1_gnn_setup():
        import jax, jax.numpy as jnp
        import numpy as np
        N_NODES = 20000
        N_EDGES = 5000
        D = 256
        N_LAYERS = 3
        BN_EPS = 1e-05
        key = jax.random.key(seed)
        ks = jax.random.split(key, 5)
        x = jax.random.normal(ks[0], (N_NODES, D), dtype=jnp.float32)
        src = jax.random.randint(ks[1], (N_EDGES,), 0, N_NODES)
        dst = jax.random.randint(ks[2], (N_EDGES,), 0, N_NODES)
        scale = 1.0 / np.sqrt(D)
        thetas = jax.random.normal(ks[3], (N_LAYERS, D, D), dtype=jnp.float32) * scale
        phis = jax.random.normal(ks[4], (N_LAYERS, D, D), dtype=jnp.float32) * scale
        gammas = jnp.ones((N_LAYERS, D), dtype=jnp.float32)
        betas = jnp.zeros((N_LAYERS, D), dtype=jnp.float32)
        return {'x': x, 'src': src, 'dst': dst, 'thetas': thetas, 'phis': phis, 'gammas': gammas, 'betas': betas}
    _L1_gnn_all = _L1_gnn_setup()
    _L1_gnn_in = {k: v for k, v in _L1_gnn_all.items() if k in ('thetas', 'phis', 'gammas', 'betas')}
    del _L1_gnn_all
    return {'x': x, 'src': src, 'dst': dst, 'L0_gnn_W': _L0_gnn_in['W'], 'L0_gnn_att_src': _L0_gnn_in['att_src'], 'L0_gnn_att_dst': _L0_gnn_in['att_dst'], 'L0_gnn_bias': _L0_gnn_in['bias'], 'L1_gnn_thetas': _L1_gnn_in['thetas'], 'L1_gnn_phis': _L1_gnn_in['phis'], 'L1_gnn_gammas': _L1_gnn_in['gammas'], 'L1_gnn_betas': _L1_gnn_in['betas']}

def reference(x, src, dst, L0_gnn_W, L0_gnn_att_src, L0_gnn_att_dst, L0_gnn_bias, L1_gnn_thetas, L1_gnn_phis, L1_gnn_gammas, L1_gnn_betas):
    import jax
    import jax.numpy as jnp

    def _L0_gnn_ref(x, edge_index, W, att_src, att_dst, bias):
        import jax, jax.numpy as jnp
        import numpy as np
        N_NODES = 50000
        N_EDGES = 25000
        H_SIZE = 256
        HEADS = 8
        HEAD_DIM = H_SIZE // HEADS
        NEG_SLOPE = 0.2
        'GATConv (concat heads) -> relu -> dropout(eval=identity).\n\n            x: [N, F]; edge_index: [2, E] with (src=row0, dst=row1) meaning message j->i.\n            '
        N = x.shape[0]
        h = jnp.einsum('nf,fhd->nhd', x, W)
        a_src = jnp.sum(h * att_src, axis=-1)
        a_dst = jnp.sum(h * att_dst, axis=-1)
        src = edge_index[0]
        dst = edge_index[1]
        e = jax.nn.leaky_relu(a_src[src] + a_dst[dst], NEG_SLOPE)
        e_max = jax.ops.segment_max(e, dst, num_segments=N)
        e_exp = jnp.exp(e - e_max[dst])
        denom = jax.ops.segment_sum(e_exp, dst, num_segments=N)
        alpha = e_exp / (denom[dst] + 1e-16)
        msg = h[src] * alpha[:, :, None]
        out = jax.ops.segment_sum(msg, dst, num_segments=N)
        out = out.reshape(N, -1) + bias
        return jax.nn.relu(out)

    def _L1_gnn_ref(x, src, dst, thetas, phis, gammas, betas):
        import jax, jax.numpy as jnp
        import numpy as np
        N_NODES = 20000
        N_EDGES = 5000
        D = 256
        N_LAYERS = 3
        BN_EPS = 1e-05
        N = x.shape[0]
        for l in range(thetas.shape[0]):
            xi = x[src]
            xj = x[dst]
            e = jax.nn.relu((xj - xi) @ thetas[l].T + xi @ phis[l].T)
            agg = jax.ops.segment_max(e, src, num_segments=N)
            agg = jnp.where(agg < -1e+30, 0.0, agg)
            mu = agg.mean(axis=0)
            var = agg.var(axis=0)
            x = jax.nn.relu((agg - mu) * jax.lax.rsqrt(var + BN_EPS) * gammas[l] + betas[l])
        return x
    edge_index = jnp.stack([src, dst])
    x = _layernorm(x + _L0_gnn_ref(x, edge_index, L0_gnn_W, L0_gnn_att_src, L0_gnn_att_dst, L0_gnn_bias), axis=-1)
    x = _layernorm(x + _L1_gnn_ref(x, src, dst, L1_gnn_thetas, L1_gnn_phis, L1_gnn_gammas, L1_gnn_betas), axis=-1)
    return x

_drawn_inputs = setup_inputs


def setup_inputs(seed=0):
    import zlib

    import numpy as np

    out = dict(_drawn_inputs(seed))
    spreads = {'L0_gnn_bias': (0.0, 0.1), 'L1_gnn_gammas': (1.0, 0.2), 'L1_gnn_betas': (0.0, 0.1)}
    factors = {'L0_gnn_att_src': 2.667, 'L0_gnn_att_dst': 6.821}
    for name, (base, spread) in spreads.items():
        noise = np.random.default_rng([zlib.crc32(name.encode()), seed]).standard_normal(out[name].shape)
        drawn = base * np.exp(spread * noise) if base else spread * noise
        out[name] = jnp.asarray(drawn.astype(out[name].dtype))
    for name, factor in factors.items():
        out[name] = (out[name] * factor).astype(out[name].dtype)
    return out
```

```python
from contextlib import ExitStack

import concourse.bass as bass
from concourse import mybir
from concourse.alu_op_type import AluOpType as ALU

ACT = mybir.ActivationFunctionType
AX = mybir.AxisListType
F32 = mybir.dt.float32
I32 = mybir.dt.int32
BF16 = mybir.dt.bfloat16
F16 = mybir.dt.float16

P = 128
N = 50000
E = 12500
D = 256
H = 8
HD = D // H
L = 3
G = 4
SUP = G * P
NS = -(-E // SUP)
EP = NS * SUP
NC = EP // P
FULL = E // P
REST = E - FULL * P
HI = -(-N // P)
HI += HI % 2
PADKEY = HI * P - 1
NONE = 30000
SKIP = 65536
EPS = 1e-5
SLOPE = 0.2
BIG = 1e30
LASTPAD = E - (NS - 1) * SUP
assert PADKEY >= N and NONE >= 2 * EP and NS % 2 == 1 and NC % 2 == 0 and HI <= 512

DR = 10
DT = N // (P * DR)
TAIL = N - DT * P * DR
assert DT % 2 == 1 and 0 < TAIL <= P


def gnn(nc, x, src, dst, w, att_src, att_dst, bias, theta_t, phi_t, gammas, betas, out):
    ctx = ExitStack()
    with ctx:
        def sem(name):
            return ctx.enter_context(nc.semaphore(name))

        def is_first(t):
            return isinstance(t, int) and t == 0

        def prev(t):
            return 0 if is_first(t) else t - 1

        def uses(phases, par):
            return phases * (NS // 2 + 1 - par)

        def sb(name, shape, dt=F32):
            return ctx.enter_context(nc.sbuf_tensor(name, shape, dt))

        table_dram = nc.dram_tensor("slot_table", (P * HI, 2), I32).ap()
        ord_dram = [nc.dram_tensor("d_order", (EP + 2, 2), I32).ap(),
                    nc.dram_tensor("s_order", (EP + 2, 4), I32).ap()]
        gidx_dram = nc.dram_tensor("d_gather", (EP, 2), I32).ap()
        same_dram = [nc.dram_tensor(f"same{k}", (EP + 1,), F32).ap() for k in range(2)]
        fidx_dram = [nc.dram_tensor(f"final{k}", (EP,), I32).ap() for k in range(2)]
        x1_dram = nc.dram_tensor("x1_rows", (2 * EP, D), F32).ap()
        x1s_dram = nc.dram_tensor("x1_src", (EP, D), F32).ap()
        nb_dram = nc.dram_tensor("neighbour", (EP, D), F32).ap()

        buf = sb("buf", [P, 10 * 1024])
        taken = [0]

        def early(shape, dt=F32):
            n = 1
            for m in shape[1:]:
                n *= m
            words = n * (2 if dt in (BF16, F16) else 4) // 4
            ap = buf[0:shape[0], taken[0]:taken[0] + words]
            taken[0] += words
            assert taken[0] <= 10 * 1024
            ap = ap if dt == F32 else ap.bitcast(dt)
            if len(shape) == 2:
                return ap
            letters = "abcd"[:len(shape) - 1]
            return ap.rearrange(f"p ({' '.join(letters)}) -> p {' '.join(letters)}", **dict(zip(letters, shape[1:])))

        ident = sb("ident", [P, P])
        iota_i = sb("iota_i", [P, HI], I32)
        iota_h = sb("iota_h", [P, HI], F16)
        iota_p = sb("iota_p", [P, 1])
        below = sb("below", [P, P])
        above = sb("above", [P, P])
        ones = sb("ones", [P, HI])
        zeros = sb("zeros", [P, 512], BF16)
        head_rows = sb("head_rows", [H, D])
        w_sb = sb("w_sb", [P, 2, D])
        att = early([P, 2, D])
        watt = early([P, 2, D])
        v_att = sb("v_att", [P, 2, 2, H])
        bias_b = sb("bias_b", [P, D])
        rbias = sb("rbias", [P, D])
        thp = sb("thp", [P, L, 2, 2, D])
        gb = sb("gb", [P, 2, L, 2])
        big = sb("big", [P, 2 * EP])
        keyrow = [big[:, k * EP:(k + 1) * EP].bitcast(I32) for k in range(2)]
        state = big[:, :].rearrange("p (j q) -> p j q", j=2)
        krow = early([NC, 2, P], I32)
        krow_f = early([NC, 2, P])
        key_i = sb("key_i", [P, 2, NC], I32)
        key_f = sb("key_f", [P, 2, NC])
        lohi_i = sb("lohi_i", [P, 2, 2, NC], I32)
        lohi = sb("lohi", [P, 2, 2, NC])
        addr = sb("addr", [P, 2, NC], I32)
        start = early([P, 2, HI])
        incl = early([P, 2, HI])
        offs = sb("offs", [P, 2])
        slots = early([P, HI, 2], I32)
        onelo = early([P, 2, 2, P], BF16)
        onehi = early([P, 2, 2, HI], BF16)
        lorow = early([P, P], I32)
        lo_t = early([P, 2, P])
        tab = early([P, 2, HI])
        junk = early([P, 512])
        rank_a = sb("rank_a", [P, 2, NC])
        rank_b = sb("rank_b", [P, 2, NC])
        rank = sb("rank", [P, 2, NC])
        rank_i = sb("rank_i", [P, 2, NC], I32)
        pay_d = early([P, NC, 2], I32)
        pay_s = early([P, NC, 4], I32)
        found = early([P, NC, 2, 2], I32)
        found_f = early([P, NC, 2, 2])
        st_i = sb("st_i", [P, 2, G], I32)
        st_pay = sb("st_pay", [P, 2, G, 4], I32)
        st_got = sb("st_got", [P, 2, G, 2], I32)
        ordt = sb("ordt", [P, NC + 2, 2], I32)
        ords = sb("ords", [P, NC, 4], I32)
        cont = sb("cont", [P, NC + 1])
        fin_f = sb("fin_f", [P, NC])
        fin_i = sb("fin_i", [P, NC], I32)
        gidx = sb("gidx", [P, NC, 2], I32)
        neg_half = sb("neg_half", [P, 2 * DR])
        sentinel = sb("sentinel", [2, 4], I32)

        hw = ctx.enter_context(nc.psum_tensor("hw", [P, 2, 512], F32))
        tpw = ctx.enter_context(nc.psum_tensor("tpw", [P, 2, 512], F32))
        bank = [hw[:, 0, :], hw[:, 1, :]] + [ctx.enter_context(nc.psum_tensor(f"bank{i}", [P, 512], F32))[:, :] for i in range(2, 6)]

        s_pad_ids = sem("pad_ids")
        s_pool_const = sem("pool_const")
        s_ids_f = sem("ids_f")
        s_ids = sem("ids")
        s_params = sem("params")
        s_hist_done = sem("hist_done")
        s_row_offsets = sem("row_offsets")
        s_setup = sem("setup")
        s_row_totals = sem("row_totals")
        s_slots_ready = sem("slots_ready")
        s_ranked = sem("ranked")
        s_prefix = sem("prefix")
        s_table_copied = sem("table_copied")
        s_table_set = sem("table_set")
        s_sentinels = sem("sentinels")
        s_table_stored = sem("table_stored")
        s_slot_kept = sem("slot_kept")
        s_found_f = sem("found_f")
        s_order_ready = sem("order_ready")
        s_order_masks = sem("order_masks")
        s_masks_stored = sem("masks_stored")
        s_order = [sem("order_0"), sem("order_1")]
        s_gat_idx = sem("gat_idx")
        s_pay_s = sem("pay_s")
        s_weights_ready = sem("weights_ready")
        s_conv_idx = sem("conv_idx")
        s_x1_ready = sem("x1_ready")
        s_gat_sums = sem("gat_sums")
        s_gat_rden = sem("gat_rden")
        s_gat_out = sem("gat_out")
        s_gat_h_kept = sem("gat_h_kept")
        s_carry_zero = sem("carry_zero")
        s_conv_squared = sem("conv_squared")
        s_bn_rstd = sem("bn_rstd")
        s_bn_rstd_eps = sem("bn_rstd_eps")
        s_bn_var = sem("bn_var")
        s_back_scan = sem("back_scan")
        s_conv_ends = sem("conv_ends")
        s_back_carry = sem("back_carry")
        s_back_mask = [sem("back_mask_0"), sem("back_mask_1")]
        s_affine = sem("affine")
        s_conv_scan = sem("conv_scan")
        s_nb_ready = sem("nb_ready")
        s_nb_kept = sem("nb_kept")
        s_c_steps = sem("c_steps")
        s_c_turned = sem("c_turned")
        s_ids_turned = sem("ids_turned")
        s_hist_used = [sem("hist_used_0"), sem("hist_used_1")]
        s_hist_onehot = sem("hist_onehot")
        s_table_updated = [sem("table_updated_0"), sem("table_updated_1")]
        s_rank_onehot = sem("rank_onehot")
        s_looked_up = sem("looked_up")
        s_rank_parts = sem("rank_parts")
        s_scattered = [sem("scattered_0"), sem("scattered_1")]
        s_staged = sem("staged")
        s_gat_negmask = sem("gat_negmask")
        s_gat_normed = sem("gat_normed")
        s_gat_got = [sem("gat_got_0"), sem("gat_got_1")]
        s_gat_staged = sem("gat_staged")
        s_gat_turned = sem("gat_turned")
        s_gat_stat = sem("gat_stat")
        s_gat_mv = sem("gat_mv")
        s_gat_kept = sem("gat_kept")
        s_gat_score = sem("gat_score")
        s_gat_exp = sem("gat_exp")
        s_gat_den = sem("gat_den")
        s_gat_num = sem("gat_num")
        s_gat_args = sem("gat_args")
        s_gat_spread = sem("gat_spread")
        s_gat_nbias = sem("gat_nbias")
        s_gat_mask = [sem("gat_mask_0"), sem("gat_mask_1")]
        s_gat_logits = sem("gat_logits")
        s_gat_leak = sem("gat_leak")
        s_gat_max = sem("gat_max")
        s_gat_arg = sem("gat_arg")
        s_gat_den_rows = sem("gat_den_rows")
        s_gat_rows = sem("gat_rows")
        s_gat_stored = [sem("gat_stored_0"), sem("gat_stored_1")]
        s_gat_recip = sem("gat_recip")
        s_gat_bias = sem("gat_bias")
        s_gat_rstd = sem("gat_rstd")
        s_gat_rstd_eps = sem("gat_rstd_eps")
        s_conv_mask = [sem("conv_mask_0"), sem("conv_mask_1")]
        s_conv_got = [sem("conv_got_0"), sem("conv_got_1")]
        s_x1s_stored = [sem("x1s_stored_0"), sem("x1s_stored_1")]
        s_conv_turned = sem("conv_turned")
        s_conv_staged = sem("conv_staged")
        s_conv_kept = sem("conv_kept")
        s_conv_edge = sem("conv_edge")
        s_bn_steps = sem("bn_steps")
        s_flipped = sem("flipped")
        s_bn_ready = sem("bn_ready")
        s_nb_rows = sem("nb_rows")
        s_nb_stored = [sem("nb_stored_0"), sem("nb_stored_1")]
        s_x1s_ready = sem("x1s_ready")
        s_nb_got = [sem("nb_got_0"), sem("nb_got_1")]
        s_nb_staged = sem("nb_staged")
        s_dense_y = sem("dense_y")
        s_dense_normed = sem("dense_normed")
        s_dense_x = [sem("dense_x_0"), sem("dense_x_1")]
        s_dense_mv1 = sem("dense_mv1")
        s_dense_mv2 = sem("dense_mv2")
        s_dense_rstd = sem("dense_rstd")
        s_dense_rstd_eps = sem("dense_rstd_eps")
        s_dense_mr = sem("dense_mr")
        s_dense_nbias = sem("dense_nbias")
        s_dense_u = sem("dense_u")
        s_dense_r1 = sem("dense_r1")
        s_dense_r1_eps = sem("dense_r1_eps")
        s_dense_stat1 = sem("dense_stat1")
        s_dense_stored = [sem("dense_stored_0"), sem("dense_stored_1")]
        s_dense_stat2 = sem("dense_stat2")
        s_dense_done = sem("dense_done")
        s_fin_sum = sem("fin_sum")
        s_fidx_loaded = sem("fidx_loaded")
        s_fin_stat = sem("fin_stat")
        s_fin_mv = sem("fin_mv")
        s_fin_normed = sem("fin_normed")
        s_fin_done = [sem("fin_done_0"), sem("fin_done_1")]
        s_fin_staged = sem("fin_staged")
        s_fin_nbias = sem("fin_nbias")
        s_affine_last = sem("affine_last")
        s_fin_x = [sem("fin_x_0"), sem("fin_x_1")]
        s_fin_rstd = sem("fin_rstd")
        s_fin_rstd_eps = sem("fin_rstd_eps")
        s_go_pool = sem("go_pool")
        s_go_dve = sem("go_dve")
        s_go_act = sem("go_act")
        s_go_pe = sem("go_pe")
        s_go_sp = sem("go_sp")
        s_slot_staged = sem("slot_staged")
        s_slot_got = [sem("slot_got_0"), sem("slot_got_1")]
        s_gat_h = sem("gat_h")
        s_gat_msg = sem("gat_msg")
        s_conv_carry = sem("conv_carry")
        s_fin_rows = sem("fin_rows")
        s_conv_pad = sem("conv_pad")

        block = ctx.enter_context(nc.Block())

        def pairs(eng, body, count):
            body(0, 0, 0)
            body(1, 1, 0)
            n = (count - 3) // 2
            with eng.Fori(0, n) as i:
                body(2 * i + 2, 0, i + 1)
                body(2 * i + 3, 1, i + 1)
            for t in range(2 * n + 2, count):
                body(t, t % 2, t // 2)

        def lagged(eng, front, back, count):
            front(0, 0, 0)
            front(1, 1, 0)
            back(0, 0, 0)
            front(2, 0, 1)
            back(1, 1, 0)
            n = (count - 4) // 2
            with eng.Fori(0, n) as i:
                front(2 * i + 3, 1, i + 1)
                back(2 * i + 2, 0, i + 1)
                front(2 * i + 4, 0, i + 2)
                back(2 * i + 3, 1, i + 1)
            for t in range(2 * n + 3, count + 1):
                if t < count:
                    front(t, t % 2, t // 2)
                back(t - 1, (t - 1) % 2, (t - 1) // 2)


        def setup_sync(sp):
            sp.wait_ge(s_pad_ids, 4)
            for k, ids in enumerate((dst, src)):
                sp.dma_start(krow[0:FULL, k, :], ids[0:FULL * P].rearrange("(c p) -> c p", p=P)).then_inc(s_ids, 16)
                sp.dma_start(krow[FULL:FULL + 1, k, 0:REST], ids[FULL * P:E].rearrange("(a p) -> a p", a=1)).then_inc(s_ids, 16)
                sp.dma_start(keyrow[k][:, 0:E], ids.partition_broadcast(P)).then_inc(s_ids, 16)
            for o, n in ((ord_dram[0], 2), (ord_dram[1], 4)):
                sp.dma_start(o[0:1, :], sentinel[0:1, 0:n]).then_inc(s_sentinels, 16)
                sp.dma_start(o[EP + 1:EP + 2, :], sentinel[1:2, 0:n]).then_inc(s_sentinels, 16)
            sp.dma_start(w_sb[:, :, :], w.rearrange("(k p) n -> p k n", p=P)).then_inc(s_params, 16)
            sp.dma_start(att[:, 0, :], att_src.partition_broadcast(P)).then_inc(s_params, 16)
            sp.dma_start(att[:, 1, :], att_dst.partition_broadcast(P)).then_inc(s_params, 16)
            sp.dma_start(bias_b[:, :], bias.partition_broadcast(P)).then_inc(s_params, 16)
            for l in range(L):
                sp.dma_start(thp[:, l, 0, :, :], theta_t[l].rearrange("(k p) n -> p k n", p=P)).then_inc(s_params, 16)
                sp.dma_start(thp[:, l, 1, :, :], phi_t[l].rearrange("(k p) n -> p k n", p=P)).then_inc(s_params, 16)
            with nc.allow_non_contiguous_dma(reason="small"):
                for t, a in enumerate((gammas, betas)):
                    sp.dma_start(gb[:, t, :, :], a).then_inc(s_params, 16)
        PARAMS = (4 + 2 * L + 2) * 16

        def setup_pool(pl):
            for k in range(2):
                pl.memset(keyrow[k][:, :], PADKEY).then_inc(s_pad_ids, 1)
            pl.memset(krow[:, :, :], PADKEY).then_inc(s_pad_ids, 1)
            pl.memset(sentinel[:, :], -1).then_inc(s_pad_ids, 1)
            pl.iota(iota_i[:, :], pattern=[[1, HI]], base=0, channel_multiplier=0).then_inc(s_pool_const, 1)
            pl.iota(iota_p[:, :], pattern=[[0, 1]], base=0, channel_multiplier=1,
                    allow_small_or_imprecise_dtypes=True).then_inc(s_pool_const, 1)
            for t, v in ((ident, 0.0), (below, 1.0), (above, 1.0), (head_rows, 1.0), (ones, 1.0), (neg_half, -0.5)):
                pl.memset(t[:, :], v).then_inc(s_pool_const, 1)
            pl.memset(zeros[:, :], 0.0).then_inc(s_pool_const, 1)
            pl.wait_ge(s_pool_const, 9)
            pl.affine_select(out=ident[:, :], in_=ident[:, :], compare_op=ALU.not_equal, fill=1.0, base=0,
                             pattern=[[-1, P]], channel_multiplier=1).then_inc(s_pool_const, 1)
            pl.affine_select(out=below[:, :], in_=below[:, :], compare_op=ALU.is_gt, fill=0.0, base=0,
                             pattern=[[-1, P]], channel_multiplier=1).then_inc(s_pool_const, 1)
            pl.affine_select(out=above[:, :], in_=above[:, :], compare_op=ALU.is_gt, fill=0.0, base=0,
                             pattern=[[1, P]], channel_multiplier=-1).then_inc(s_pool_const, 1)
            hr = head_rows[:, :].rearrange("p (a b) -> p a b", a=H)
            pl.affine_select(out=hr, in_=hr, compare_op=ALU.is_equal, fill=0.0, base=0,
                             pattern=[[-1, H], [0, HD]], channel_multiplier=1).then_inc(s_pool_const, 1)
        POOL_CONST = 13

        def setup_pe(pe):
            pe.wait_ge(s_pool_const, POOL_CONST)
            pe.wait_ge(s_ids_f, 1)
            for k in range(2):
                pe.transpose(bank[k][:, 0:NC], krow_f[:, k, :], ident[0:NC, 0:NC]).then_inc(s_ids_turned, 1)

        def setup_dve(v):
            v.wait_ge(s_ids, 6 * 16)
            v.tensor_copy(krow_f[:, :, :], krow[:, :, :]).then_inc(s_ids_f, 1)
            v.wait_ge(s_pool_const, POOL_CONST)
            n = 0

            def s(ins):
                nonlocal n
                n += 1
                ins.then_inc(s_setup, 1)
                v.wait_ge(s_setup, n)
            s(v.tensor_copy(iota_h[:, :], iota_i[:, :]))
            for k in range(2):
                v.wait_ge(s_ids_turned, k + 1)
                s(v.tensor_copy(key_f[:, k, :], bank[k][:, 0:NC]))
                s(v.tensor_copy(key_i[:, k, :], key_f[:, k, :]))
                s(v.tensor_scalar(lohi_i[:, k, 0, :], key_i[:, k, :], P - 1, None, ALU.bitwise_and))
                s(v.tensor_scalar(lohi_i[:, k, 1, :], key_i[:, k, :], 7, None, ALU.logical_shift_right))
                s(v.tensor_copy(lohi[:, k, :, :], lohi_i[:, k, :, :]))
                s(v.scalar_tensor_tensor(addr[:, k, :], lohi[:, k, 0, :], float(HI), lohi[:, k, 1, :], ALU.mult, ALU.add))
            s(v.tensor_copy(pay_d[:, :, 0], key_i[:, 1, :]))
            s(v.tensor_copy(pay_d[:, :, 1], key_i[:, 0, :]))
            v.wait_ge(s_params, PARAMS)
            s(v.tensor_scalar(rbias[:, :], bias_b[:, :], 0.0, None, ALU.max))
            for a in range(2):
                for k in range(2):
                    s(v.tensor_tensor(watt[:, k, :], w_sb[:, k, :], att[:, a, :], ALU.mult))
                    s(v.tensor_reduce(v_att[:, a, k, :], watt[:, k, :].rearrange("p (h d) -> p h d", h=H), AX.X, ALU.add))
            for l in range(L):
                s(v.tensor_tensor(thp[:, l, 1, :, :], thp[:, l, 1, :, :], thp[:, l, 0, :, :], ALU.subtract))
            v.sem_inc(s_weights_ready, 1)

        def onehot(v, k, par, c, s_ready, value):
            v.tensor_scalar(onelo[:, par, k, :], iota_h[:, 0:P], lohi[:, k, 0, bass.ds(c, 1)], None, ALU.is_equal).then_inc(s_ready, 1)
            v.wait_ge(s_ready, value + 1)
            v.tensor_scalar(onehi[:, par, k, :], iota_h[:, :], lohi[:, k, 1, bass.ds(c, 1)], None, ALU.is_equal).then_inc(s_ready, 1)
            v.wait_ge(s_ready, value + 2)

        def hist_dve(v):
            def body(c, par, u):
                v.wait_ge(s_hist_used[par], u)
                for k in range(2):
                    onehot(v, k, par, c, s_hist_onehot, 4 * c + 2 * k)
            pairs(v, body, NC)
            n = 0

            def s(ins):
                nonlocal n
                n += 1
                ins.then_inc(s_prefix, 1)
                v.wait_ge(s_prefix, n)
            v.wait_ge(s_hist_done, 1)
            for k in range(2):
                cnt = bank[k][:, 0:HI]
                s(v.tensor_tensor_scan(incl[:, k, :], ones[:, :], cnt, 0.0, ALU.mult, ALU.add))
            v.sem_inc(s_row_totals, 1)
            v.wait_ge(s_row_offsets, 1)
            s(v.tensor_copy(offs[:, :], bank[2][:, 0:2]))
            for k in range(2):
                cnt = bank[k][:, 0:HI]
                s(v.tensor_scalar(incl[:, k, :], incl[:, k, :], offs[:, k:k + 1], None, ALU.add))
                s(v.tensor_tensor(start[:, k, :], incl[:, k, :], cnt, ALU.subtract))
                s(v.tensor_scalar(junk[:, 0:HI], cnt, 0.0, float(NONE), ALU.is_equal, ALU.mult))
                s(v.scalar_tensor_tensor(slots[:, :, k], incl[:, k, :], 1.0, junk[:, 0:HI], ALU.subtract, ALU.add))
            v.sem_inc(s_slots_ready, 1)

        def hist_pe(pe):
            pe.wait_ge(s_setup, 13)
            for k in range(2):
                pe.matmul(bank[k][:, 0:HI], zeros[:, 0:P], zeros[:, 0:HI], start=True, stop=False, skip_group_check=True)

            def body(c, par, u):
                pe.wait_ge(s_hist_onehot, 4 * c + 4)
                for k in range(2):
                    m = pe.matmul(bank[k][:, 0:HI], onelo[:, par, k, :], onehi[:, par, k, :], start=False, stop=False,
                                  skip_group_check=True)
                m.then_inc(s_hist_used[par], 1)
            pairs(pe, body, NC)
            for k in range(2):
                m = pe.matmul(bank[k][:, 0:HI], zeros[:, 0:P], zeros[:, 0:HI], start=False, stop=True, skip_group_check=True)
            m.then_inc(s_hist_done, 1)
            pe.wait_ge(s_row_totals, 1)
            pe.matmul(bank[2][:, 0:2], above[:, :], incl[:, :, HI - 1], start=True, stop=True).then_inc(s_row_offsets, 1)

        def hist_sync(sp):
            sp.wait_ge(s_slots_ready, 1)
            sp.dma_start(table_dram.rearrange("(p r) c -> p r c", p=P), slots[:, :, :]).then_inc(s_table_stored, 16)

        def rank_dve(v, k):
            u0 = k * NC // 2
            c0 = k * NC
            def front(c, par, u):
                v.wait_ge(s_table_updated[par], u0 + u)
                if k or not is_first(c):
                    v.wait_ge(s_rank_parts, 2 * (c0 + c) - 2)
                onehot(v, k, par, c, s_rank_onehot, 4 * (c0 + c))
                v.tensor_scalar(lorow[:, :], keyrow[k][:, bass.ds(c * P, P)], P - 1, None, ALU.bitwise_and).then_inc(s_rank_onehot, 1)
                v.wait_ge(s_rank_onehot, 4 * (c0 + c) + 3)
                v.tensor_scalar(lo_t[:, par, :], lorow[:, :], iota_p[:, 0:1], None, ALU.is_equal).then_inc(s_rank_onehot, 1)
                v.wait_ge(s_rank_onehot, 4 * (c0 + c) + 4)

            def back(c, par, u):
                v.wait_ge(s_looked_up, c0 + c + 1)
                v.scalar_tensor_tensor(junk[:, 0:HI], onehi[:, par, k, :], 1.0, bank[1 + par][:, 0:HI], ALU.mult, ALU.mult,
                                              accum_out=rank_a[:, k, bass.ds(c, 1)]).then_inc(s_rank_parts, 1)
                v.wait_ge(s_rank_parts, 2 * (c0 + c) + 1)
                v.scalar_tensor_tensor(junk[:, 0:P], keyrow[k][:, bass.ds(c * P, P)], key_f[:, k, bass.ds(c, 1)], below[:, :],
                                              ALU.is_equal, ALU.mult, accum_out=rank_b[:, k, bass.ds(c, 1)]).then_inc(s_rank_parts, 1)
                v.wait_ge(s_rank_parts, 2 * (c0 + c) + 2)
            lagged(v, front, back, NC)
            v.tensor_tensor(rank[:, k, :], rank_a[:, k, :], rank_b[:, k, :], ALU.add).then_inc(s_ranked, 1)
            v.wait_ge(s_ranked, 2 * k + 1)
            v.tensor_scalar(rank_i[:, k, :], rank[:, k, :], 1.0, None, ALU.add).then_inc(s_ranked, 1)
            v.wait_ge(s_ranked, 2 * k + 2)

        def rank_pe(pe, k):
            c0 = k * NC
            pe.wait_ge(s_prefix, 10)
            pe.wait_ge(s_table_copied, c0)
            pe.matmul(bank[0][:, 0:HI], ident[:, :], start[:, k, :], start=True, stop=False,
                      skip_group_check=True).then_inc(s_table_set, 1)

            def body(c, par, u):
                pe.wait_ge(s_rank_onehot, 4 * (c0 + c) + 4)
                pe.wait_ge(s_table_copied, c0 + c + 1)
                pe.matmul(bank[1 + par][:, 0:HI], lo_t[:, par, :], tab[:, par, :], start=True, stop=True).then_inc(s_looked_up, 1)
                pe.matmul(bank[0][:, 0:HI], onelo[:, par, k, :], onehi[:, par, k, :], start=False, stop=False,
                          skip_group_check=True).then_inc(s_table_updated[par], 1)
            pairs(pe, body, NC)

        def rank_act(a, k):
            u0 = k * NC // 2
            c0 = k * NC
            a.wait_ge(s_table_set, k + 1)

            def body(c, par, u):
                if par == 0:
                    a.wait_ge(s_table_updated[1], u0 + u)
                else:
                    a.wait_ge(s_table_updated[0], u0 + u + 1)
                a.activation(tab[:, par, :], bank[0][:, 0:HI], ACT.Copy).then_inc(s_table_copied, 1)
                a.wait_ge(s_table_copied, c0 + c + 1)
            pairs(a, body, NC)


        def scatter_pool(pl, k):
            width = (2, 4)[k]
            pay = (pay_d, pay_s)[k]
            pl.wait_ge(s_ranked, 2 * k + 2)
            pl.wait_ge(s_sentinels, 64)
            if k:
                pl.wait_ge(s_pay_s, 4)
            g0, u0 = k * NS, (k * (NS // 2 + 1), k * (NS // 2))

            def body(g, par, u):
                pl.wait_ge(s_scattered[par], 64 * (u + u0[par]))
                pl.sem_inc(s_go_pool, 1)
                pl.tensor_copy(st_i[:, par, :], rank_i[:, k, bass.ds(g * G, G)]).then_inc(s_staged, 1)
                pl.tensor_copy(st_pay[:, par, :, 0:width], pay[:, bass.ds(g * G, G), :]).then_inc(s_staged, 1)
                pl.wait_ge(s_staged, 2 * (g + g0) + 2)
                pl.sem_inc(s_go_pool, 1)
                for s in range(G):
                    pl.indirect_dma_start(ord_dram[k][:, :], bass.IndirectOffsetOnAxis(ap=st_i[:, par, s:s + 1], axis=0),
                                          st_pay[:, par, s, 0:width], None).then_inc(s_scattered[par], 16)
            pairs(pl, body, NS)
            pl.wait_ge(s_scattered[0], 64 * (u0[0] + NS // 2 + 1))
            pl.wait_ge(s_scattered[1], 64 * (u0[1] + NS // 2))
            pl.sem_inc(s_go_pool, 1)
            pl.sem_inc(s_order_ready, 1)


        def look_up_slots(pl):
            pl.wait_ge(s_table_stored, 16)
            for a in range(2):
                def body(g, par, u):
                    u = u + a * (NS // 2 + 1 - par)
                    g1 = g + a * NS
                    pl.wait_ge(s_slot_kept, g1)
                    pl.sem_inc(s_go_pool, 1)
                    pl.tensor_copy(st_i[:, par, :], addr[:, a, bass.ds(g * G, G)]).then_inc(s_slot_staged, 1)
                    pl.wait_ge(s_slot_staged, g1 + 1)
                    pl.sem_inc(s_go_pool, 1)
                    for s in range(G):
                        pl.indirect_dma_start(st_got[:, par, s, :], None, table_dram[:, :],
                                              bass.IndirectOffsetOnAxis(ap=st_i[:, par, s:s + 1], axis=0)).then_inc(s_slot_got[par], 16)
                    pl.wait_ge(s_slot_got[par], 64 * (u + 1))
                    pl.sem_inc(s_go_pool, 1)
                    pl.tensor_copy(found[:, bass.ds(g * G, G), a, :], st_got[:, par, :, :]).then_inc(s_slot_kept, 1)
                pairs(pl, body, NS)

        def payload_s(v):
            v.wait_ge(s_slot_kept, 2 * NS)
            v.wait_ge(s_ranked, 4)
            n = 0

            def s(ins):
                nonlocal n
                n += 1
                ins.then_inc(s_pay_s, 1)
                v.wait_ge(s_pay_s, n)
            v.tensor_copy(found_f[:, :, :, :], found[:, :, :, :]).then_inc(s_found_f, 1)
            v.wait_ge(s_found_f, 1)
            s(v.tensor_copy(pay_s[:, :, 0], key_i[:, 1, :]))
            s(v.scalar_tensor_tensor(pay_s[:, :, 1], rank[:, 0, :], float(EP), found_f[:, :, 1, 0], ALU.add, ALU.min))
            s(v.tensor_copy(pay_s[:, :, 2], found_f[:, :, 0, 0]))
            s(v.tensor_scalar(pay_s[:, :, 3], found_f[:, :, 0, 1], float(EP - 1), None, ALU.min))

        def order_sync(sp, k):
            o = ord_dram[k]
            w_ = (2, 4)[k]
            t = ordt if k == 0 else ords

            sp.wait_ge(s_order_ready, k + 1)
            kc = 1 - k
            if k == 0:
                sp.dma_start(ordt[:, 1:NC + 1, :], o[1:EP + 1, :].rearrange("(p r) c -> p r c", p=P)).then_inc(s_order[k], 16)
                sp.dma_start(ordt[:, 0:1, :], o[0:EP, :].rearrange("(p r) c -> p r c", p=P)[:, 0:1, :]).then_inc(s_order[k], 16)
                sp.dma_start(ordt[:, NC + 1:NC + 2, :], o[2:EP + 2, :].rearrange("(p r) c -> p r c", p=P)[:, NC - 1:NC, :]).then_inc(s_order[k], 16)
            else:
                sp.wait_ge(s_order_masks, 3)
                sp.dma_start(ords[:, :, :], o[1:EP + 1, :].rearrange("(p r) c -> p r c", p=P)).then_inc(s_order[k], 16)
                sp.dma_start(ordt[:, 0:1, :], o[0:EP, :].rearrange("(p r) c -> p r c", p=P)[:, 0:1, 0:2]).then_inc(s_order[k], 16)
                sp.dma_start(ordt[:, NC + 1:NC + 2, :], o[2:EP + 2, :].rearrange("(p r) c -> p r c", p=P)[:, NC - 1:NC, 0:2]).then_inc(s_order[k], 16)
            sp.wait_ge(s_order_masks, (3, 7)[k])
            sp.dma_start(same_dram[k][0:EP].rearrange("(p r) -> p r", p=P), cont[:, 0:NC]).then_inc(s_masks_stored, 16)
            sp.dma_start(same_dram[k][EP:EP + 1].rearrange("(a r) -> a r", a=1), cont[P - 1:P, NC:NC + 1]).then_inc(s_masks_stored, 16)
            sp.dma_start(fidx_dram[k].rearrange("(p r) -> p r", p=P), fin_i[:, :]).then_inc(s_masks_stored, 16)
            if k == 0:
                sp.dma_start(gidx_dram.rearrange("(p r) c -> p r c", p=P), gidx[:, :, :]).then_inc(s_masks_stored, 16)
            sp.wait_ge(s_masks_stored, (64, 112)[k])

        def order_dve(v, k):
            v.wait_ge(s_order[k], 48)
            n = 4 * k

            def s(ins):
                nonlocal n
                n += 1
                ins.then_inc(s_order_masks, 1)
                v.wait_ge(s_order_masks, n)
            if k == 0:
                s(v.tensor_scalar(gidx[:, :, :], ordt[:, 1:NC + 1, :], float(N - 1), None, ALU.min))
            else:
                v.wait_ge(s_masks_stored, 64)
                s(v.tensor_copy(ordt[:, 1:NC + 1, 0], ords[:, :, 0]))
            kc = 1 - k
            s(v.tensor_tensor(cont[:, :], ordt[:, 1:NC + 2, kc], ordt[:, 0:NC + 1, kc], ALU.is_equal))
            s(v.scalar_tensor_tensor(fin_i[:, :], cont[:, 1:NC + 1], float(SKIP), ordt[:, 1:NC + 1, kc], ALU.mult, ALU.add))
            if k == 0:
                v.sem_inc(s_order_masks, 1)
                v.wait_ge(s_order_masks, 4)

        rows_in = buf[:, 0:4096].rearrange("p (b a g f) -> p b a g f", b=2, a=2, g=G)
        rows_out = buf[:, 4096:8192].rearrange("p (b a g f) -> p b a g f", b=2, a=2, g=G)
        turned = buf[:, 8192:10240].rearrange("p (a j q) -> p a j q", a=2, j=2)
        wide = [hw, tpw]
        mask = sb("mask", [P, 2, SUP])
        mask_n = sb("mask_n", [P, 2, SUP])
        idx_all = sb("idx_all", [P, NS, G, 4], I32)
        idx_d = sb("idx_d", [P, NS, G, 2], I32)
        idx = sb("idx", [P, 2, G, 4], I32)
        stat = sb("stat", [P, 2 * DR, 6])
        mv = sb("mv", [P, 2 * DR, 2])
        rstd = sb("rstd", [P, 2, 2 * DR])
        nbias = sb("nbias", [P, 2, 2 * DR])
        tiny = sb("tiny", [P, G, H])
        rden = sb("rden", [P, G, H])

        def inv_std(pl, out_ap, var_ap, s_eps_added, s_done, eps_count):
            pl.tensor_scalar(out_ap, var_ap, EPS, None, ALU.add).then_inc(s_eps_added, 1)
            pl.wait_ge(s_eps_added, eps_count)
            pl.sem_inc(s_go_pool, 1)
            flat = out_ap.shape[1]
            pl.tensor_tensor(out_ap, out_ap, neg_half[0:out_ap.shape[0], 0:flat], ALU.pow).then_inc(s_done, 1)

        used = [0]

        def carve(n, rows=P):
            used[0] += n
            assert used[0] <= EP
            return big[0:rows, used[0] - n:used[0]]

        score = carve(SUP, H)
        negm = carve(SUP, H)
        runmax = [carve(SUP + 1, H) for _ in range(2)]
        args = carve(2 * SUP, H).rearrange("p (a q) -> p a q", a=2)
        expd = [carve(2 * SUP, H).rearrange("p (a q) -> p a q", a=2) for _ in range(2)]
        den = [carve(SUP, H) for _ in range(2)]
        h_sb = [carve(2 * SUP).rearrange("p (j q) -> p j q", j=2) for _ in range(2)]
        num = [carve(2 * SUP).rearrange("p (j q) -> p j q", j=2) for _ in range(2)]
        msg = carve(SUP)

        def by_slot(ap, s):
            return ap.rearrange("f (p g) -> f g p", g=G)[:, s, :]

        def turn_rows(pe, dst_bank, rows, j):
            for s in range(G):
                m = pe.transpose(dst_bank[:, s * P:(s + 1) * P], rows[:, s, j * P:(j + 1) * P], ident[:, :])
            return m

        def keep_turned(a, out_ap, bank_ap):
            return a.activation(out_ap.rearrange("f (p g) -> f g p", g=G), bank_ap.rearrange("f (g p) -> f g p", g=G), ACT.Copy)

        def norm_stats(v, s_stat, s_mv, rows, n, t):
            for r in range(n):
                v.bn_stats(stat[:rows[r].shape[0], r, :], rows[r]).then_inc(s_stat, 1)
                v.wait_ge(s_stat, n * t + r + 1)
            v.sem_inc(s_go_dve, 1)
            for r in range(n):
                m = v.bn_aggr(mv[:rows[r].shape[0], r, :], stat[:rows[r].shape[0], r, :])
                m.then_inc(s_mv, 1)

        def gat_sync(sp):
            sp.wait_ge(s_masks_stored, 64)
            sp.dma_start(idx_d[:, :, :, :], gidx_dram.rearrange("(t p g) c -> p t g c", p=P, g=G)).then_inc(s_gat_idx, 16)

            def front(t, par, u):
                sp.wait_ge(s_gat_negmask, prev(t))
                sp.dma_start(mask[0:H, par, :], same_dram[0][bass.ds(t * SUP, SUP)].partition_broadcast(H)).then_inc(s_gat_mask[par], 16)

            def back(t, par, u):
                sp.wait_ge(s_gat_normed, 8 * (t + 1))
                for a in range(2):
                    sp.dma_start(x1_dram[bass.ds(a * EP + t * SUP, SUP), :].rearrange("(p g) f -> p g f", g=G),
                                 rows_out[:, par, a, :, :]).then_inc(s_gat_stored[par], 16)
            lagged(sp, front, back, NS)
            sp.wait_ge(s_gat_stored[0], 32 * (NS // 2 + 1))
            sp.wait_ge(s_gat_stored[1], 32 * (NS // 2))
            sp.sem_inc(s_x1_ready, 1)

        def gat_pool(pl):
            pl.wait_ge(s_gat_idx, 16)
            pl.wait_ge(s_table_updated[0], NC)
            pl.wait_ge(s_table_updated[1], NC)
            pl.wait_ge(s_table_copied, 2 * NC)
            pl.wait_ge(s_pay_s, 4)

            def front(t, par, u):
                pl.wait_ge(s_gat_got[par], 128 * u)
                pl.wait_ge(s_gat_sums, 2 * prev(t))
                pl.sem_inc(s_go_pool, 1)
                pl.tensor_copy(idx[:, par, :, 0:2], idx_d[:, bass.ds(t, 1), :, :].rearrange("p a g c -> p (a g) c")).then_inc(s_gat_staged, 1)
                pl.wait_ge(s_gat_staged, t + 1)
                pl.wait_ge(s_gat_turned, 4 * prev(t))
                pl.sem_inc(s_go_pool, 1)
                for a in range(2):
                    for s in range(G):
                        pl.indirect_dma_start(rows_in[:, par, a, s, :], None, x[:, :],
                                              bass.IndirectOffsetOnAxis(ap=idx[:, par, s, a:a + 1], axis=0)).then_inc(s_gat_got[par], 16)

            def back(t, par, u):
                pl.wait_ge(s_gat_mv, 8 * (t + 1))
                pl.wait_ge(s_gat_normed, 8 * prev(t))
                pl.sem_inc(s_go_pool, 1)
                inv_std(pl, rstd[:, par, 0:8], mv[:, 0:8, 1], s_gat_rstd_eps, s_gat_rstd, t + 1)
            lagged(pl, front, back, NS)

        def gat_pe(pe):
            pe.wait_ge(s_weights_ready, 1)
            banks = wide[1]

            def front(t, par, u):
                pe.wait_ge(s_gat_got[par], 128 * (u + 1))
                pe.wait_ge(s_gat_out, prev(t))
                for n in range(4):
                    a, j = n // 2, n % 2
                    if n >= 2:
                        pe.wait_ge(s_gat_kept, 4 * t + n - 1)
                    turn_rows(pe, banks[:, j, :], rows_in[:, par, a, :, :], j).then_inc(s_gat_turned, 1)
                pe.wait_ge(s_gat_kept, 4 * t + 4)
                pe.wait_ge(s_gat_score, t)
                for n in range(4):
                    a, k = n // 2, n % 2
                    m = pe.matmul(bank[2][0:H, :], v_att[:, a, k, :], turned[:, a, k, :], start=(n == 0), stop=(n == 3))
                m.then_inc(s_gat_logits, 1)
                pe.wait_ge(s_gat_h_kept, 2 * t)
                for j in range(2):
                    for k in range(2):
                        m = pe.matmul(wide[0][:, j, :], w_sb[:, k, j * P:(j + 1) * P], turned[:, 0, k, :], start=(k == 0), stop=(k == 1))
                    m.then_inc(s_gat_h, 1)

            def back(t, par, u):
                pe.wait_ge(s_gat_exp, t + 1)
                for j in range(2):
                    pe.wait_ge(s_gat_num, 2 * t + j)
                    pe.matmul(bank[4][:, :], head_rows[:, j * P:(j + 1) * P], expd[par][:, 1, :], start=True, stop=True)
                    pe.matmul(bank[5][:, :], head_rows[:, j * P:(j + 1) * P], expd[par][:, 0, :], start=True, stop=True).then_inc(s_gat_spread, 1)
                pe.wait_ge(s_gat_den, t + 1)
                pe.wait_ge(s_gat_rden, t)
                pe.sem_inc(s_go_pe, 1)
                for s in range(G):
                    m = pe.transpose(bank[3][:, s * H:(s + 1) * H], by_slot(den[par], s), ident[0:H, 0:H])
                m.then_inc(s_gat_den_rows, 1)
                pe.wait_ge(s_gat_num, 2 * t + 2)
                for s in range(G):
                    for j in range(2):
                        m = pe.transpose(banks[:, s // 2, (s % 2) * D + j * P:(s % 2) * D + (j + 1) * P], by_slot(num[par][:, j, :], s), ident[:, :])
                m.then_inc(s_gat_rows, 1)
            lagged(pe, front, back, NS)

        def gat_act(act):
            def front(t, par, u):
                for n in range(4):
                    a, j = n // 2, n % 2
                    if n == 0:
                        act.wait_ge(s_gat_h, 2 * t)
                    act.wait_ge(s_gat_turned, 4 * t + n + 1)
                    keep_turned(act, turned[:, a, j, :], wide[1][:, j, :]).then_inc(s_gat_kept, 1)
                act.wait_ge(s_gat_num, 2 * prev(t))
                for j in range(2):
                    act.wait_ge(s_gat_h, 2 * t + j + 1)
                    act.activation(h_sb[par][:, j, :], wide[0][:, j, :], ACT.Copy).then_inc(s_gat_h_kept, 1)
                act.wait_ge(s_gat_args, t + 1)
                act.wait_ge(s_gat_spread, 2 * prev(t))
                act.wait_ge(s_gat_den, prev(t))
                act.activation(expd[par][:, :, :], args[:, :, :], ACT.Exp).then_inc(s_gat_exp, 1)

            def back(t, par, u):
                act.wait_ge(s_gat_nbias, t + 1)
                for n in range(8):
                    o = rows_out[:, par, n // G, n % G, :]
                    act.activation(o, o, ACT.Identity, scale=rstd[:, par, n:n + 1], bias=nbias[:, par, n:n + 1]).then_inc(s_gat_normed, 1)
            lagged(act, front, back, NS)

        def gat_dve(v):
            def front(t, par, u):
                v.wait_ge(s_gat_mask[par], 16 * (u + 1))
                v.tensor_scalar(negm, mask[0:H, par, :], BIG, -BIG, ALU.mult, ALU.add).then_inc(s_gat_negmask, 1)
                v.wait_ge(s_gat_negmask, t + 1)
                v.wait_ge(s_gat_logits, t + 1)
                v.tensor_scalar(score, bank[2][0:H, :], SLOPE, None, ALU.mult).then_inc(s_gat_leak, 1)
                v.wait_ge(s_gat_leak, t + 1)
                v.tensor_tensor(score, score, bank[2][0:H, :], ALU.max).then_inc(s_gat_score, 1)
                v.wait_ge(s_gat_score, t + 1)
                if is_first(t):
                    v.memset(runmax[0][:, 0:1], 0.0).then_inc(s_gat_max, 1)
                    v.wait_ge(s_gat_max, 1)
                else:
                    v.tensor_copy(runmax[par][:, 0:1], runmax[1 - par][:, SUP:SUP + 1]).then_inc(s_gat_max, 1)
                    v.wait_ge(s_gat_max, 2 * t + 1)
                v.tensor_tensor_scan(runmax[par][:, 1:SUP + 1], negm, score, runmax[par][:, 0:1], ALU.add, ALU.max).then_inc(s_gat_max, 1)
                v.wait_ge(s_gat_max, 2 * t + 2)
                v.wait_ge(s_gat_exp, t)
                v.tensor_tensor(args[:, 0, :], runmax[par][:, 0:SUP], negm, ALU.add).then_inc(s_gat_arg, 1)
                v.wait_ge(s_gat_arg, 2 * t + 1)
                v.tensor_tensor(args[:, 0, :], args[:, 0, :], runmax[par][:, 1:SUP + 1], ALU.subtract).then_inc(s_gat_arg, 1)
                v.wait_ge(s_gat_arg, 2 * t + 2)
                v.tensor_tensor(args[:, 1, :], score, runmax[par][:, 1:SUP + 1], ALU.subtract).then_inc(s_gat_args, 1)
                v.wait_ge(s_gat_args, t + 1)

            def back(t, par, u):
                first = is_first(t)
                v.wait_ge(s_gat_exp, t + 1)
                v.wait_ge(s_gat_den_rows, prev(t))
                v.tensor_tensor_scan(den[par], expd[par][:, 0, :], expd[par][:, 1, :],
                                            0.0 if first else den[1 - par][:, SUP - 1:SUP], ALU.mult, ALU.add).then_inc(s_gat_den, 1)
                v.wait_ge(s_gat_den, t + 1)
                v.wait_ge(s_gat_rows, prev(t))
                for j in range(2):
                    v.wait_ge(s_gat_h_kept, 2 * t + j + 1)
                    v.wait_ge(s_gat_spread, 2 * t + j + 1)
                    v.tensor_tensor(msg, h_sb[par][:, j, :], bank[4][:, :], ALU.mult).then_inc(s_gat_msg, 1)
                    v.wait_ge(s_gat_msg, 2 * t + j + 1)
                    v.tensor_tensor_scan(num[par][:, j, :], bank[5][:, :], msg,
                                                0.0 if first else num[1 - par][:, j, SUP - 1:SUP], ALU.mult, ALU.add).then_inc(s_gat_num, 1)
                    v.wait_ge(s_gat_num, 2 * t + j + 1)
                ya, yb = rows_out[:, par, 0, :, :], rows_out[:, par, 1, :, :]
                v.wait_ge(s_gat_stored[par], 32 * u)
                v.tensor_tensor(yb, rows_in[:, par, 0, :, :], rbias[:, :].unsqueeze(1).to_broadcast([P, G, D]), ALU.add).then_inc(s_gat_sums, 1)
                v.wait_ge(s_gat_sums, 2 * t + 1)
                v.wait_ge(s_gat_den_rows, t + 1)
                v.tensor_scalar(tiny[:, :, :], bank[3][:, 0:G * H].rearrange("p (g h) -> p g h", g=G), 1e-16, None, ALU.add).then_inc(s_gat_rden, 1)
                v.wait_ge(s_gat_rden, t + 1)
                v.reciprocal(rden[:, :, :], tiny[:, :, :]).then_inc(s_gat_recip, 1)
                v.wait_ge(s_gat_recip, t + 1)
                v.wait_ge(s_gat_rows, t + 1)
                v.tensor_tensor(ya.rearrange("p g (h d) -> p (g h) d", h=H), wide[1][:, :, :].rearrange("p b (h d) -> p (b h) d", d=HD),
                                       rden[:, :, :].rearrange("p g h -> p (g h)").unsqueeze(2).to_broadcast([P, G * H, HD]), ALU.mult).then_inc(s_gat_out, 1)
                v.wait_ge(s_gat_out, t + 1)
                v.tensor_tensor(ya, ya, bias_b[:, :].unsqueeze(1).to_broadcast([P, G, D]), ALU.add).then_inc(s_gat_bias, 1)
                v.wait_ge(s_gat_bias, t + 1)
                v.scalar_tensor_tensor(ya, ya, 0.0, rows_in[:, par, 1, :, :], ALU.max, ALU.add).then_inc(s_gat_sums, 1)
                v.wait_ge(s_gat_sums, 2 * t + 2)
                v.wait_ge(s_gat_rstd, t)
                norm_stats(v, s_gat_stat, s_gat_mv, [rows_out[:, par, n // G, n % G, :] for n in range(8)], 8, t)
                v.wait_ge(s_gat_rstd, t + 1)
                v.wait_ge(s_gat_mv, 8 * (t + 1))
                v.scalar_tensor_tensor(nbias[:, par, 0:8], mv[:, 0:8, 0], -1.0, rstd[:, par, 0:8], ALU.mult, ALU.mult).then_inc(s_gat_nbias, 1)
                v.wait_ge(s_gat_nbias, t + 1)
            lagged(v, front, back, NS)

        part = sb("part", [P, 2, 2, NS])
        tot = sb("tot", [P, 2, 2])
        bn = sb("bn", [P, 4, 2])
        bn_scale = sb("bn_scale", [P, 2])
        bn_shift = sb("bn_shift", [P, 2])
        ends = sb("ends", [P, 2, SUP])
        flipped = sb("flipped", [P, 2, 2, SUP])
        back_carry = sb("back_carry", [P, 2])
        c_rows = sb("c_rows", [P, D])
        sq = sb("sq", [P, SUP])

        def half(j, t):
            return state[:, j, bass.ds(t * SUP, SUP)]

        def conv_loads(sp, l):
            def load(t, par, u):
                tl = t + l * NS
                sp.wait_ge(s_conv_ends, 2 * (l * NS + prev(t)))
                sp.dma_start(mask[:, par, :], same_dram[1][bass.ds(t * SUP, SUP)].partition_broadcast(P)).then_inc(s_conv_mask[par], 16)
                sp.dma_start(mask_n[:, par, :], same_dram[1][bass.ds(t * SUP + 1, SUP)].partition_broadcast(P)).then_inc(s_conv_mask[par], 16)
            return load

        def conv_max(v, l):
            def body(t, par, u):
                tl = t + l * NS
                first, last = is_first(t), isinstance(t, int) and t == NS - 1
                v.wait_ge(s_conv_mask[par], 32 * (u + uses(l, par) + 1))
                for j in range(2):
                    v.wait_ge(s_conv_edge, 2 * tl + 2)
                    v.tensor_tensor_scan(half(j, t), mask[:, par, :], wide[par][:, j, :], state_carry[:, j:j + 1], ALU.mult, ALU.max).then_inc(s_conv_scan, 1)
                    v.wait_ge(s_conv_scan, 2 * tl + j + 1)
                    v.tensor_scalar(state_carry[:, j:j + 1], state[:, j, bass.ds(t * SUP + SUP - 1, 1)], 1.0, None, ALU.mult).then_inc(s_conv_carry, 1)
                    v.wait_ge(s_conv_carry, 2 * tl + j + 1)
                    if last:
                        v.memset(state[:, j, E:EP], 0.0).then_inc(s_conv_pad, 1)
                        v.wait_ge(s_conv_pad, 2 * l + j + 1)
                    if l or not is_first(t):
                        v.wait_ge(s_conv_squared, 2 * tl + j - 1)
                    v.sem_inc(s_go_dve, 1)
                    v.scalar_tensor_tensor(ends[:, j, :], mask_n[:, par, :], 0.0, half(j, t), ALU.is_equal, ALU.mult,
                                                  accum_out=part[:, 0, j, bass.ds(t, 1)]).then_inc(s_conv_ends, 1)
                    v.wait_ge(s_conv_ends, 2 * tl + j + 1)
            return body

        def conv_squares(a, l):
            def body(t, par, u):
                tl = t + l * NS
                for j in range(2):
                    a.wait_ge(s_conv_ends, 2 * tl + j + 1)
                    a.sem_inc(s_go_act, 1)
                    a.activation(sq[:, :], ends[:, j, :], ACT.Square, accum_out=part[:, 1, j, bass.ds(t, 1)]).then_inc(s_conv_squared, 1)
                    a.wait_ge(s_conv_squared, 2 * tl + j + 1)
            return body
        state_carry = sb("state_carry", [P, 2])

        def first_sync(sp):
            sp.wait_ge(s_masks_stored, 112)
            sp.dma_start(idx_all[:, :, :, :], ord_dram[1][1:EP + 1, :].rearrange("(t p g) c -> p t g c", p=P, g=G)).then_inc(s_conv_idx, 16)
            load = conv_loads(sp, 0)

            def back(t, par, u):
                sp.wait_ge(s_conv_got[par], 128 * (u + 1))
                sp.dma_start(x1s_dram[bass.ds(t * SUP, SUP), :].rearrange("(p g) f -> p g f", g=G), rows_in[:, par, 0, :, :]).then_inc(s_x1s_stored[par], 16)
            lagged(sp, load, back, NS)
            sp.wait_ge(s_x1s_stored[0], 16 * (NS // 2 + 1))
            sp.wait_ge(s_x1s_stored[1], 16 * (NS // 2))
            sp.sem_inc(s_x1s_ready, 1)

        def first_pool(pl):
            pl.wait_ge(s_conv_idx, 16)
            pl.wait_ge(s_x1_ready, 1)
            pl.wait_ge(s_gat_got[0], 128 * (NS // 2 + 1))
            pl.wait_ge(s_gat_got[1], 128 * (NS // 2))
            pl.wait_ge(s_gat_sums, 2 * NS)

            def body(t, par, u):
                pl.wait_ge(s_conv_got[par], 128 * u)
                pl.wait_ge(s_x1s_stored[par], 16 * u)
                pl.wait_ge(s_conv_turned, 4 * prev(t))
                pl.sem_inc(s_go_pool, 1)
                pl.tensor_copy(idx[:, par, :, :], idx_all[:, bass.ds(t, 1), :, :].rearrange("p a g c -> p (a g) c")).then_inc(s_conv_staged, 1)
                pl.wait_ge(s_conv_staged, t + 1)
                pl.sem_inc(s_go_pool, 1)
                for a in range(2):
                    for s in range(G):
                        pl.indirect_dma_start(rows_in[:, par, a, s, :], None, x1_dram[:, :],
                                              bass.IndirectOffsetOnAxis(ap=idx[:, par, s, a + 1:a + 2], axis=0)).then_inc(s_conv_got[par], 16)
            pairs(pl, body, NS)

        def first_pe(pe):
            pe.wait_ge(s_gat_rden, NS)
            pe.wait_ge(s_gat_out, NS)
            pe.wait_ge(s_gat_h_kept, 2 * NS)

            def body(t, par, u):
                pe.wait_ge(s_conv_got[par], 128 * (u + 1))
                pe.wait_ge(s_conv_kept, 4 * t)
                for n in range(4):
                    turn_rows(pe, bank[2 + n][:, :], rows_in[:, par, n // 2, :, :], n % 2).then_inc(s_conv_turned, 1)
                pe.wait_ge(s_conv_kept, 4 * t + 4)
                pe.wait_ge(s_conv_scan, 2 * prev(t))
                for j in range(2):
                    for n in range(4):
                        a, k = n // 2, n % 2
                        m = pe.matmul(wide[par][:, j, :], thp[:, 0, 1 - a, k, j * P:(j + 1) * P], turned[:, a, k, :], start=(n == 0), stop=(n == 3))
                    m.then_inc(s_conv_edge, 1)
            pairs(pe, body, NS)

        def first_act(a):
            square = conv_squares(a, 0)

            def front(t, par, u):
                a.wait_ge(s_conv_edge, 2 * t)
                for n in range(4):
                    a.wait_ge(s_conv_turned, 4 * t + n + 1)
                    keep_turned(a, turned[:, n // 2, n % 2, :], bank[2 + n][:, :]).then_inc(s_conv_kept, 1)
            lagged(a, front, square, NS)

        def first_dve(v):
            v.memset(state_carry[:, :], 0.0).then_inc(s_carry_zero, 1)
            v.wait_ge(s_carry_zero, 1)
            pairs(v, conv_max(v, 0), NS)

        def norm_dve(v, l):
            v.wait_ge(s_conv_squared, 2 * NS * (l + 1))
            n = 7 * l

            def s(ins):
                nonlocal n
                n += 1
                ins.then_inc(s_bn_steps, 1)
                v.wait_ge(s_bn_steps, n)
            s(v.tensor_reduce(tot[:, :, :], part[:, :, :, :], AX.X, ALU.add))
            s(v.tensor_scalar(bn[:, 0:2, :], tot[:, :, :], 1.0 / N, None, ALU.mult))
            s(v.tensor_tensor(bn[:, 2, :], bn[:, 0, :], bn[:, 0, :], ALU.mult))
            s(v.tensor_tensor(bn[:, 2, :], bn[:, 1, :], bn[:, 2, :], ALU.subtract))
            v.sem_inc(s_bn_var, 1)
            v.wait_ge(s_bn_rstd, l + 1)
            s(v.tensor_tensor(bn_scale[:, :], bn[:, 3, :], gb[:, 0, l, :], ALU.mult))
            s(v.tensor_tensor(bn[:, 2, :], bn[:, 0, :], bn_scale[:, :], ALU.mult))
            s(v.tensor_tensor(bn_shift[:, :], gb[:, 1, l, :], bn[:, 2, :], ALU.subtract))
            v.sem_inc(s_bn_ready, 1)

        def norm_pool(pl, l):
            pl.wait_ge(s_bn_var, l + 1)
            inv_std(pl, bn[:, 3, :], bn[:, 2, :], s_bn_rstd_eps, s_bn_rstd, l + 1)


        def back_load(sp, l, t, par, u):
            tl = l * NS + t
            sp.wait_ge(s_back_scan, 2 * (l * NS + prev(t)))
            sp.wait_ge(s_conv_ends, 2 * NS * (l + 1))
            sp.sem_inc(s_go_sp, 1)
            sp.dma_start(mask[:, par, :], same_dram[1][bass.ds((NS - 1 - t) * SUP + 1, SUP)].partition_broadcast(P)).then_inc(s_back_mask[par], 16)

        def flip(a, l, t, par, u):
            tl = l * NS + t
            a.wait_ge(s_back_carry, 2 * (l * NS + prev(t)))
            a.sem_inc(s_go_act, 1)
            for j in range(2):
                a.activation(flipped[:, par, j, ::-1], half(j, NS - 1 - t), ACT.Copy).then_inc(s_flipped, 1)

        def spread(v, l, t, par, u):
            tl = l * NS + t
            first = is_first(t)
            v.wait_ge(s_back_mask[par], 16 * (u + uses(l, par) + 1))
            for j in range(2):
                v.wait_ge(s_flipped, 2 * tl + j + 1)
                v.tensor_tensor_scan(flipped[:, par, j, :], mask[:, par, ::-1], flipped[:, par, j, :],
                                            0.0 if first else back_carry[:, j:j + 1], ALU.mult, ALU.max).then_inc(s_back_scan, 1)
                v.wait_ge(s_back_scan, 2 * tl + j + 1)
                v.tensor_copy(back_carry[:, j:j + 1], flipped[:, par, j, SUP - 1:SUP]).then_inc(s_back_carry, 1)
                v.wait_ge(s_back_carry, 2 * tl + j + 1)

        def affine(a, l, t, par, u, keep):
            tl = l * NS + t
            for j in range(2):
                a.wait_ge(s_back_scan, 2 * tl + j + 1)
                a.wait_ge(s_bn_ready, l + 1)
                a.sem_inc(s_go_act, 1)
                outs = [turned[:, par, j, :]] + ([half(j, NS - 1 - t)] if keep else [])
                for o in outs:
                    a.activation(o, flipped[:, par, j, ::-1], ACT.Relu, scale=bn_scale[:, j:j + 1],
                                 bias=bn_shift[:, j:j + 1]).then_inc(s_affine if keep else s_affine_last, 1)

        def neighbour_sync(sp, l):
            t0 = (l - 1) * NS
            def back(t, par, u):
                sp.wait_ge(s_nb_kept, 2 * (t0 + t) + 2)
                sp.sem_inc(s_go_sp, 1)
                sp.dma_start(nb_dram[bass.ds((NS - 1 - t) * SUP, SUP), :].rearrange("(p g) f -> p g f", g=G),
                             rows_out[:, par, 0, :, :]).then_inc(s_nb_stored[par], 16)
            lagged(sp, lambda t, par, u: back_load(sp, l - 1, t, par, u), back, NS)
            sp.wait_ge(s_nb_stored[0], 16 * (uses(l - 1, 0) + NS // 2 + 1))
            sp.wait_ge(s_nb_stored[1], 16 * (uses(l - 1, 1) + NS // 2))
            sp.sem_inc(s_nb_ready, 1)

        def neighbour_dve(v, l):
            pairs(v, lambda t, par, u: spread(v, l - 1, t, par, u), NS)
            v.wait_ge(s_affine, 4 * NS * l)
            v.memset(state_carry[:, :], 0.0).then_inc(s_carry_zero, 1)
            v.wait_ge(s_carry_zero, l + 1)

        def neighbour_act(a, l):
            t0 = (l - 1) * NS
            def front(t, par, u):
                if is_first(t):
                    a.wait_ge(s_conv_edge, 2 * NS * l)
                flip(a, l - 1, t, par, u)

            def back(t, par, u):
                a.wait_ge(s_nb_rows, t0 + prev(t))
                a.sem_inc(s_go_act, 1)
                affine(a, l - 1, t, par, u, True)
                a.wait_ge(s_nb_stored[par], 16 * (u + uses(l - 1, par)))
                a.wait_ge(s_nb_rows, t0 + t + 1)
                a.sem_inc(s_go_act, 1)
                for b in range(2):
                    a.activation(rows_out[:, par, 0, 2 * b:2 * b + 2, :].rearrange("p g f -> p (g f)"), wide[par][:, b, :], ACT.Copy).then_inc(s_nb_kept, 1)
            lagged(a, front, back, NS)

        def neighbour_pe(pe, l):
            t0 = (l - 1) * NS
            pe.wait_ge(s_conv_scan, 2 * NS * l)

            def body(t, par, u):
                pe.wait_ge(s_affine, 4 * (t0 + t) + 4)
                pe.wait_ge(s_nb_kept, 2 * (t0 + prev(t)))
                for s in range(G):
                    for k in range(2):
                        m = pe.matmul(wide[par][:, s // 2, (s % 2) * D:(s % 2 + 1) * D], by_slot(turned[:, par, k, :], s), thp[:, l, 0, k, :],
                                      start=(k == 0), stop=(k == 1), skip_group_check=True)
                m.then_inc(s_nb_rows, 1)
            pairs(pe, body, NS)


        def edge_sync(sp, l):
            sp.wait_ge(s_back_scan, 2 * NS * l)
            pairs(sp, conv_loads(sp, l), NS)

        def edge_pool(pl, l):
            pl.wait_ge(s_nb_ready, l)
            if l == 1:
                pl.wait_ge(s_conv_got[0], 128 * (NS // 2 + 1))
                pl.wait_ge(s_conv_got[1], 128 * (NS // 2))
                pl.wait_ge(s_x1s_ready, 1)
                pl.wait_ge(s_conv_turned, 4 * NS)

            def body(t, par, u):
                tl = (l - 1) * NS + t
                pl.wait_ge(s_nb_got[par], 64 * (u + uses(l - 1, par)))
                pl.wait_ge(s_conv_edge, 2 * (l * NS + prev(t)))
                pl.sem_inc(s_go_pool, 1)
                pl.tensor_copy(idx[:, par, :, :], idx_all[:, bass.ds(t, 1), :, :].rearrange("p a g c -> p (a g) c")).then_inc(s_nb_staged, 1)
                pl.wait_ge(s_nb_staged, tl + 1)
                pl.sem_inc(s_go_pool, 1)
                for s in range(G):
                    pl.indirect_dma_start(rows_in[:, par, 0, s, :], None, nb_dram[:, :],
                                          bass.IndirectOffsetOnAxis(ap=idx[:, par, s, 3:4], axis=0)).then_inc(s_nb_got[par], 16)
            pairs(pl, body, NS)

        def edge_pe(pe, l):
            pe.wait_ge(s_nb_kept, 2 * NS * l)
            pe.wait_ge(s_affine, 4 * NS * l)

            def body(t, par, u):
                tl = l * NS + t
                pe.wait_ge(s_conv_scan, 2 * (l * NS + prev(t)))
                for j in range(2):
                    for k in range(2):
                        pe.matmul(wide[par][:, j, :], thp[:, l, 1, k, j * P:(j + 1) * P], half(k, t), start=(k == 0), stop=False, skip_group_check=True)
                    if j == 0:
                        pe.wait_ge(s_nb_got[par], 64 * (u + uses(l - 1, par) + 1))
                    for s in range(G):
                        m = pe.matmul(by_slot(wide[par][:, j, :], s), rows_in[:, par, 0, s, j * P:(j + 1) * P], ident[:, :],
                                      start=False, stop=(s == G - 1), skip_group_check=True)
                    m.then_inc(s_conv_edge, 1)
            pairs(pe, body, NS)

        def edge_act(a, l):
            pairs(a, conv_squares(a, l), NS)

        def edge_dve(v, l):
            pairs(v, conv_max(v, l), NS)



        cvec = sb("cvec", [P, 2])
        cmat = sb("cmat", [P, P])
        fidx = sb("fidx", [P, 2, NS, G], I32)
        last = L - 1

        def last_state_dve(v):
            v.tensor_scalar(cvec[:, :], bn_shift[:, :], 0.0, None, ALU.max).then_inc(s_c_steps, 1)
            v.wait_ge(s_c_steps, 1)
            for j in range(2):
                v.wait_ge(s_c_turned, j)
                v.tensor_scalar(cmat[:, :], ones[:, 0:P], cvec[:, j:j + 1], None, ALU.mult).then_inc(s_c_steps, 1)
                v.wait_ge(s_c_steps, 2 + j)
            v.wait_ge(s_c_turned, 2)
            v.tensor_copy(c_rows[:, :], bank[2][:, 0:D]).then_inc(s_c_steps, 1)
            v.wait_ge(s_c_steps, 4)

        def last_state_pe(pe):
            for j in range(2):
                pe.wait_ge(s_c_steps, 2 + j)
                pe.matmul(bank[2][:, j * P:(j + 1) * P], cmat[:, :], ident[:, :], start=True, stop=True).then_inc(s_c_turned, 1)

        x_tile = buf[:, 0:2 * DR * D].rearrange("p (b r f) -> p b r f", b=2, r=DR)
        y_tile = buf[:, 2 * DR * D:4 * DR * D].rearrange("p (b r f) -> p b r f", b=2, r=DR)
        stat1 = sb("stat1", [P, DR, 6])
        mv1 = sb("mv1", [P, 2, DR, 2])
        r1 = sb("r1", [P, 2, DR])

        def tile_rows(t):
            if isinstance(t, int) and t == DT:
                return slice(DT * P * DR, N), TAIL, 1
            return bass.ds(t * P * DR, P * DR), P, DR

        def dense_sync(sp):
            sp.wait_ge(s_conv_squared, 2 * NS * L)
            for k in range(2):
                sp.dma_start(fidx[:, k, :, :], fidx_dram[k].rearrange("(t p g) -> p t g", p=P, g=G)).then_inc(s_fidx_loaded, 16)

            def front(t, par, u):
                rows, p, r = tile_rows(t)
                sp.wait_ge(s_dense_y, prev(t))
                sp.dma_start(x_tile[0:p, par, 0:r, :], x[rows, :].rearrange("(p r) f -> p r f", r=r)).then_inc(s_dense_x[par], 16)

            def back(t, par, u):
                rows, p, r = tile_rows(t)
                sp.wait_ge(s_dense_normed, DR * t + r)
                sp.dma_start(out[rows, :].rearrange("(p r) f -> p r f", r=r), y_tile[0:p, par, 0:r, :]).then_inc(s_dense_stored[par], 16)
            lagged(sp, front, back, DT + 1)
            sp.wait_ge(s_dense_stored[0], 16 * (DT // 2 + 1))
            sp.wait_ge(s_dense_stored[1], 16 * (DT // 2 + 1))
            sp.sem_inc(s_dense_done, 1)

        def dense_pool(pl):
            def front(t, par, u):
                rows, p, r = tile_rows(t)
                pl.wait_ge(s_dense_x[par], 16 * (u + 1))
                pl.sem_inc(s_go_pool, 1)
                pl.tensor_tensor(x_tile[0:p, par, 0:r, :], x_tile[0:p, par, 0:r, :], rbias[0:p, :].unsqueeze(1).to_broadcast([p, r, D]), ALU.add).then_inc(s_dense_u, 1)
                pl.wait_ge(s_dense_mv1, DR * t + r)
                pl.wait_ge(s_dense_y, prev(t))
                pl.sem_inc(s_go_pool, 1)
                inv_std(pl, r1[0:p, par, 0:r], mv1[0:p, par, 0:r, 1], s_dense_r1_eps, s_dense_r1, t + 1)

            def back(t, par, u):
                rows, p, r = tile_rows(t)
                pl.wait_ge(s_dense_mv2, DR * t + r)
                pl.wait_ge(s_dense_normed, DR * prev(t))
                pl.sem_inc(s_go_pool, 1)
                inv_std(pl, rstd[0:p, par, 0:r], mv[0:p, 0:r, 1], s_dense_rstd_eps, s_dense_rstd, t + 1)
                pl.wait_ge(s_dense_rstd, t + 1)
                pl.sem_inc(s_go_pool, 1)
                pl.tensor_tensor(nbias[0:p, par, 0:r], mv[0:p, 0:r, 0], rstd[0:p, par, 0:r], ALU.mult).then_inc(s_dense_mr, 1)
                pl.wait_ge(s_dense_mr, t + 1)
                pl.sem_inc(s_go_pool, 1)
                pl.tensor_scalar(nbias[0:p, par, 0:r], nbias[0:p, par, 0:r], -1.0, None, ALU.mult).then_inc(s_dense_nbias, 1)
            lagged(pl, front, back, DT + 1)

        def dense_act(a):
            def body(t, par, u):
                rows, p, r = tile_rows(t)
                a.wait_ge(s_dense_nbias, t + 1)
                for n in range(r):
                    o = y_tile[0:p, par, n, :]
                    a.activation(o, o, ACT.Identity, scale=rstd[0:p, par, n:n + 1], bias=nbias[0:p, par, n:n + 1]).then_inc(s_dense_normed, 1)
            pairs(a, body, DT + 1)

        def dense_dve(v):
            def front(t, par, u):
                rows, p, r = tile_rows(t)
                v.wait_ge(s_dense_u, t + 1)
                v.wait_ge(s_dense_r1, prev(t))
                v.wait_ge(s_dense_mv1, DR * t)
                for n in range(r):
                    m = v.bn_stats(stat1[0:p, n, :], x_tile[0:p, par, n, :])
                    m.then_inc(s_dense_stat1, 1)
                v.wait_ge(s_dense_stat1, DR * t + r)
                v.sem_inc(s_go_dve, 1)
                for n in range(r):
                    v.bn_aggr(mv1[0:p, par, n, :], stat1[0:p, n, :]).then_inc(s_dense_mv1, 1)

            def back(t, par, u):
                rows, p, r = tile_rows(t)
                v.wait_ge(s_dense_r1, t + 1)
                v.wait_ge(s_dense_stored[par], 16 * u)
                for n in range(r):
                    m = v.scalar_tensor_tensor(y_tile[0:p, par, n, :], x_tile[0:p, par, n, :], r1[0:p, par, n:n + 1], c_rows[0:p, :], ALU.mult, ALU.add)
                    if n == r - 1:
                        m.then_inc(s_dense_y, 1)
                v.wait_ge(s_dense_y, t + 1)
                v.wait_ge(s_dense_mv2, DR * t)
                v.sem_inc(s_go_dve, 1)
                for n in range(r):
                    v.bn_stats(stat[0:p, n, :], y_tile[0:p, par, n, :]).then_inc(s_dense_stat2, 1)
                v.wait_ge(s_dense_stat2, DR * t + r)
                v.wait_ge(s_dense_nbias, t)
                v.sem_inc(s_go_dve, 1)
                for n in range(r):
                    v.bn_aggr(mv[0:p, n, :], stat[0:p, n, :]).then_inc(s_dense_mv2, 1)
            lagged(v, front, back, DT + 1)

        def final_sync(sp, kind):
            f0 = kind * NS
            if kind == 0:
                sp.wait_ge(s_dense_done, 1)

            def front(t, par, u):
                sp.wait_ge(s_fin_sum, f0 + prev(t))
                sp.sem_inc(s_go_sp, 1)
                r = t if kind == 0 else NS - 1 - t
                source = x1_dram if kind == 0 else x1s_dram
                sp.dma_start(rows_in[:, par, 0, :, :], source[bass.ds(r * SUP, SUP), :].rearrange("(p g) f -> p g f", g=G)).then_inc(s_fin_x[par], 16)
                if kind:
                    back_load(sp, last, t, par, u)
            pairs(sp, front, NS)
            if kind:
                sp.wait_ge(s_fin_done[0], 64 * (2 * (NS // 2) + 2))
                sp.wait_ge(s_fin_done[1], 64 * 2 * (NS // 2))

        def final_pool(pl, kind):
            f0 = kind * NS
            if kind == 0:
                pl.wait_ge(s_fidx_loaded, 32)
                pl.wait_ge(s_dense_done, 1)

            def front(t, par, u):
                tf = f0 + t
                pl.wait_ge(s_fin_mv, G * (tf + 1))
                pl.wait_ge(s_fin_normed, G * (f0 + prev(t)))
                pl.sem_inc(s_go_pool, 1)
                inv_std(pl, rstd[:, par, 0:G], mv[:, 0:G, 1], s_fin_rstd_eps, s_fin_rstd, tf + 1)
                r = t if kind == 0 else NS - 1 - t
                pl.wait_ge(s_fin_done[par], 64 * (u + uses(kind, par)))
                pl.sem_inc(s_go_pool, 1)
                pl.tensor_copy(idx[:, par, :, 0], fidx[:, kind, bass.ds(r, 1), :].rearrange("p a g -> p (a g)")).then_inc(s_fin_staged, 1)

            def back(t, par, u):
                tf = f0 + t
                pl.wait_ge(s_fin_normed, G * (tf + 1))
                pl.wait_ge(s_fin_staged, tf + 1)
                pl.sem_inc(s_go_pool, 1)
                for s in range(G):
                    pl.indirect_dma_start(out[:, :], bass.IndirectOffsetOnAxis(ap=idx[:, par, s, 0:1], axis=0), rows_out[:, par, 0, s, :], None,
                                          bounds_check=N - 1, oob_is_err=False).then_inc(s_fin_done[par], 16)
            lagged(pl, front, back, NS)
            pl.wait_ge(s_fin_done[0], 64 * (kind + 1) * (NS // 2 + 1))
            pl.wait_ge(s_fin_done[1], 64 * (kind + 1) * (NS // 2))

        def final_act(a, kind):
            f0 = kind * NS
            def front(t, par, u):
                if kind:
                    flip(a, last, t, par, u)

            def back(t, par, u):
                if kind:
                    a.wait_ge(s_fin_rows, prev(t))
                    a.sem_inc(s_go_act, 1)
                    affine(a, last, t, par, u, False)
                a.wait_ge(s_fin_nbias, f0 + t + 1)
                for n in range(G):
                    o = rows_out[:, par, 0, n, :]
                    a.activation(o, o, ACT.Identity, scale=rstd[:, par, n:n + 1], bias=nbias[:, par, n:n + 1]).then_inc(s_fin_normed, 1)
            lagged(a, front, back, NS)

        def final_pe(pe, kind):
            f0 = kind * NS
            def body(t, par, u):
                pe.wait_ge(s_affine_last, 2 * t + 2)
                pe.wait_ge(s_fin_sum, f0 + prev(t))
                for s in range(G):
                    for k in range(2):
                        m = pe.transpose(wide[par][:, s // 2, (s % 2) * D + k * P:(s % 2) * D + (k + 1) * P], by_slot(turned[:, par, k, :], s), ident[:, :])
                m.then_inc(s_fin_rows, 1)
            pairs(pe, body, NS)

        def final_dve(v, kind):
            f0 = kind * NS
            if kind == 0:
                v.wait_ge(s_dense_done, 1)

            def body(t, par, u):
                tf = f0 + t
                y = rows_out[:, par, 0, :, :]
                if kind:
                    spread(v, last, t, par, u)
                    v.wait_ge(s_fin_rows, t + 1)
                v.wait_ge(s_fin_x[par], 16 * (u + uses(kind, par) + 1))
                v.wait_ge(s_fin_done[par], 64 * (u + uses(kind, par)))
                other = wide[par][:, :, :].rearrange("p b (s f) -> p (b s) f", f=D) if kind else c_rows[:, :].unsqueeze(1).to_broadcast([P, G, D])
                v.tensor_tensor(y, other, rows_in[:, par, 0, :, :], ALU.add).then_inc(s_fin_sum, 1)
                v.wait_ge(s_fin_sum, tf + 1)
                norm_stats(v, s_fin_stat, s_fin_mv, [rows_out[:, par, 0, n, :] for n in range(G)], G, tf)
                v.wait_ge(s_fin_rstd, tf + 1)
                v.wait_ge(s_fin_mv, G * (tf + 1))
                v.scalar_tensor_tensor(nbias[:, par, 0:G], mv[:, 0:G, 0], -1.0, rstd[:, par, 0:G], ALU.mult, ALU.mult).then_inc(s_fin_nbias, 1)
                v.wait_ge(s_fin_nbias, tf + 1)
            pairs(v, body, NS)

        @block.sync
        def _(sp):
            setup_sync(sp)
            hist_sync(sp)
            for k in range(2):
                order_sync(sp, k)
            gat_sync(sp)
            first_sync(sp)
            for l in range(1, L):
                neighbour_sync(sp, l)
                edge_sync(sp, l)
            dense_sync(sp)
            for kind in range(2):
                final_sync(sp, kind)

        @block.gpsimd
        def _(pool):
            setup_pool(pool)
            scatter_pool(pool, 0)
            look_up_slots(pool)
            scatter_pool(pool, 1)
            gat_pool(pool)
            first_pool(pool)
            norm_pool(pool, 0)
            for l in range(1, L):
                edge_pool(pool, l)
                norm_pool(pool, l)
            dense_pool(pool)
            for kind in range(2):
                final_pool(pool, kind)

        @block.scalar
        def _(act):
            for k in range(2):
                rank_act(act, k)
            gat_act(act)
            first_act(act)
            for l in range(1, L):
                neighbour_act(act, l)
                edge_act(act, l)
            dense_act(act)
            for kind in range(2):
                final_act(act, kind)

        @block.vector
        def _(dve):
            setup_dve(dve)
            hist_dve(dve)
            rank_dve(dve, 0)
            order_dve(dve, 0)
            rank_dve(dve, 1)
            payload_s(dve)
            order_dve(dve, 1)
            gat_dve(dve)
            first_dve(dve)
            norm_dve(dve, 0)
            for l in range(1, L):
                neighbour_dve(dve, l)
                edge_dve(dve, l)
                norm_dve(dve, l)
            last_state_dve(dve)
            dense_dve(dve)
            for kind in range(2):
                final_dve(dve, kind)

        @block.tensor
        def _(pe):
            setup_pe(pe)
            hist_pe(pe)
            for k in range(2):
                rank_pe(pe, k)
            gat_pe(pe)
            first_pe(pe)
            for l in range(1, L):
                neighbour_pe(pe, l)
                edge_pe(pe, l)
            last_state_pe(pe)
            final_pe(pe, 1)


def layout(x, src, dst, L0_gnn_W, L0_gnn_att_src, L0_gnn_att_dst, L0_gnn_bias,
           L1_gnn_thetas, L1_gnn_phis, L1_gnn_gammas, L1_gnn_betas):
    import numpy as np
    by_feature = lambda a: np.ascontiguousarray(np.asarray(a).reshape(L, 2, P).transpose(2, 0, 1))
    turned = lambda a: np.ascontiguousarray(np.asarray(a).transpose(0, 2, 1))
    return {
        "x": np.ascontiguousarray(x), "src": np.ascontiguousarray(src), "dst": np.ascontiguousarray(dst),
        "w": np.ascontiguousarray(L0_gnn_W).reshape(D, D), "att_src": np.ascontiguousarray(L0_gnn_att_src).reshape(D),
        "att_dst": np.ascontiguousarray(L0_gnn_att_dst).reshape(D), "bias": np.ascontiguousarray(L0_gnn_bias),
        "theta_t": turned(L1_gnn_thetas), "phi_t": turned(L1_gnn_phis),
        "gammas": by_feature(L1_gnn_gammas), "betas": by_feature(L1_gnn_betas),
    }


def kernel(x, src, dst, L0_gnn_W, L0_gnn_att_src, L0_gnn_att_dst, L0_gnn_bias,
           L1_gnn_thetas, L1_gnn_phis, L1_gnn_gammas, L1_gnn_betas):
    import numpy as np
    import concourse.bacc as bacc
    from concourse.bass_utils import run_bass_kernel_spmd

    nc = bacc.Bacc("TRN2", target_bir_lowering=False, num_devices=1)
    arrays = layout(x, src, dst, L0_gnn_W, L0_gnn_att_src, L0_gnn_att_dst, L0_gnn_bias,
                    L1_gnn_thetas, L1_gnn_phis, L1_gnn_gammas, L1_gnn_betas)
    args = [nc.dram_tensor(name, a.shape, mybir.dt.from_np(a.dtype), kind="ExternalInput").ap() for name, a in arrays.items()]
    out = nc.dram_tensor("out", (N, D), F32, kind="ExternalOutput").ap()
    gnn(nc, *args, out)
    run = run_bass_kernel_spmd(nc, [arrays], core_ids=[0])
    return run.results[0]["out"]
```

```python
from contextlib import ExitStack

import concourse.bass as bass
from concourse import mybir
from concourse.alu_op_type import AluOpType as ALU

ACT = mybir.ActivationFunctionType
AX = mybir.AxisListType
F32 = mybir.dt.float32
I32 = mybir.dt.int32
BF16 = mybir.dt.bfloat16
F16 = mybir.dt.float16

P = 128
N = 50000
E = 12500
D = 256
H = 8
HD = D // H
L = 3
G = 4
SUP = G * P
NS = -(-E // SUP)
EP = NS * SUP
NC = EP // P
FULL = E // P
REST = E - FULL * P
HI = -(-N // P)
HI += HI % 2
PADKEY = HI * P - 1
NONE = 30000
SKIP = 65536
EPS = 1e-5
SLOPE = 0.2
BIG = 1e30
LASTPAD = E - (NS - 1) * SUP
assert PADKEY >= N and NONE >= 2 * EP and NS % 2 == 1 and NC % 2 == 0 and HI <= 512

DR = 5
DT = N // (P * DR)
TAIL = N - DT * P * DR
RING = 4
assert 0 < TAIL <= P and TAIL % 16 == 0


def gnn(nc, x, src, dst, w, att_src, att_dst, bias, theta_t, phi_t, gammas, betas, out):
    ctx = ExitStack()
    with ctx:
        def sem(name):
            return ctx.enter_context(nc.semaphore(name))

        def is_first(t):
            return isinstance(t, int) and t == 0

        def prev(t):
            return 0 if is_first(t) else t - 1

        def uses(phases, par):
            return phases * (NS // 2 + 1 - par)

        def sb(name, shape, dt=F32):
            return ctx.enter_context(nc.sbuf_tensor(name, shape, dt))

        table_dram = nc.dram_tensor("slot_table", (P * HI, 2), I32).ap()
        ord_dram = [nc.dram_tensor("d_order", (EP + 2, 2), I32).ap(),
                    nc.dram_tensor("s_order", (EP + 2, 4), I32).ap()]
        gidx_dram = nc.dram_tensor("d_gather", (EP, 2), I32).ap()
        same_dram = [nc.dram_tensor(f"same{k}", (EP + 1,), F32).ap() for k in range(2)]
        fidx_dram = [nc.dram_tensor(f"final{k}", (EP,), I32).ap() for k in range(2)]
        x1_dram = nc.dram_tensor("x1_rows", (2 * EP, D), F32).ap()
        x1s_dram = nc.dram_tensor("x1_src", (EP, D), F32).ap()
        nb_dram = nc.dram_tensor("neighbour", (EP, D), F32).ap()

        buf = sb("buf", [P, 10 * 1024])
        taken = [0]

        def early(shape, dt=F32):
            n = 1
            for m in shape[1:]:
                n *= m
            words = n * (2 if dt in (BF16, F16) else 4) // 4
            ap = buf[0:shape[0], taken[0]:taken[0] + words]
            taken[0] += words
            assert taken[0] <= 10 * 1024
            ap = ap if dt == F32 else ap.bitcast(dt)
            if len(shape) == 2:
                return ap
            letters = "abcd"[:len(shape) - 1]
            return ap.rearrange(f"p ({' '.join(letters)}) -> p {' '.join(letters)}", **dict(zip(letters, shape[1:])))

        ident = sb("ident", [P, P])
        iota_i = sb("iota_i", [P, HI], I32)
        iota_h = sb("iota_h", [P, HI], F16)
        iota_p = sb("iota_p", [P, 1])
        below = sb("below", [P, P])
        above = sb("above", [P, P])
        ones = sb("ones", [P, HI])
        zeros = sb("zeros", [P, 512], BF16)
        head_rows = sb("head_rows", [H, D])
        w_sb = sb("w_sb", [P, 2, D])
        att = early([P, 2, D])
        watt = early([P, 2, D])
        v_att = sb("v_att", [P, 2, 2, H])
        bias_b = sb("bias_b", [P, D])
        rbias = sb("rbias", [P, D])
        thp = sb("thp", [P, L, 2, 2, D])
        gb = sb("gb", [P, 2, L, 2])
        big = sb("big", [P, 2 * EP])
        keyrow = [big[:, k * EP:(k + 1) * EP].bitcast(I32) for k in range(2)]
        state = big[:, :].rearrange("p (j q) -> p j q", j=2)
        krow = early([NC, 2, P], I32)
        krow_f = early([NC, 2, P])
        key_i = sb("key_i", [P, 2, NC], I32)
        key_f = sb("key_f", [P, 2, NC])
        lohi_i = sb("lohi_i", [P, 2, 2, NC], I32)
        lohi = sb("lohi", [P, 2, 2, NC])
        addr = sb("addr", [P, 2, NC], I32)
        start = early([P, 2, HI])
        incl = early([P, 2, HI])
        offs = sb("offs", [P, 2])
        slots = early([P, HI, 2], I32)
        onelo = early([P, 2, 2, P], BF16)
        onehi = early([P, 2, 2, HI], BF16)
        lorow = early([P, P], I32)
        lo_t = early([P, 2, P])
        tab = early([P, 2, HI])
        junk = early([P, HI + P])
        rank_a = sb("rank_a", [P, 2, NC])
        rank_b = sb("rank_b", [P, 2, NC])
        rank = sb("rank", [P, 2, NC])
        rank_i = sb("rank_i", [P, 2, NC], I32)
        pay_d = early([P, NC, 2], I32)
        pay_s = early([P, NC, 4], I32)
        found = early([P, NC, 2, 2], I32)
        found_f = early([P, NC, 2, 2])
        st_i = sb("st_i", [P, 2, G], I32)
        st_pay = sb("st_pay", [P, 2, G, 4], I32)
        st_got = sb("st_got", [P, 2, G, 2], I32)
        ordt = sb("ordt", [P, NC + 2, 2], I32)
        ords = sb("ords", [P, NC, 4], I32)
        cont = sb("cont", [P, NC + 1])
        fin_f = sb("fin_f", [P, NC])
        fin_i = sb("fin_i", [P, NC], I32)
        gidx = sb("gidx", [P, NC, 2], I32)
        neg_half = sb("neg_half", [P, 8])
        eps_b = sb("eps_b", [P, 1])
        sentinel = sb("sentinel", [2, 4], I32)

        hw = ctx.enter_context(nc.psum_tensor("hw", [P, 2, 512], F32))
        tpw = ctx.enter_context(nc.psum_tensor("tpw", [P, 2, 512], F32))
        bank = [hw[:, 0, :], hw[:, 1, :]] + [ctx.enter_context(nc.psum_tensor(f"bank{i}", [P, 512], F32))[:, :] for i in range(2, 6)]

        s_pad_ids = sem("pad_ids")
        s_pool_const = sem("pool_const")
        s_ids_f = sem("ids_f")
        s_ids = sem("ids")
        s_params = sem("params")
        s_hist_done = sem("hist_done")
        s_row_offsets = sem("row_offsets")
        s_setup = sem("setup")
        s_ranked = sem("ranked")
        s_prefix = sem("prefix")
        s_table_copied = sem("table_copied")
        s_table_set = sem("table_set")
        s_sentinels = sem("sentinels")
        s_table_stored = sem("table_stored")
        s_slot_kept = sem("slot_kept")
        s_found_f = sem("found_f")
        s_order_ready = sem("order_ready")
        s_order_masks = sem("order_masks")
        s_masks_stored = sem("masks_stored")
        s_order = [sem("order_0"), sem("order_1")]
        s_gat_idx = sem("gat_idx")
        s_pay_s = sem("pay_s")
        s_weights_ready = sem("weights_ready")
        s_conv_idx = sem("conv_idx")
        s_x1_ready = sem("x1_ready")
        s_gat_sums = sem("gat_sums")
        s_gat_rden = sem("gat_rden")
        s_gat_out = sem("gat_out")
        s_gat_h_kept = sem("gat_h_kept")
        s_carry_zero = sem("carry_zero")
        s_conv_squared = sem("conv_squared")
        s_bn_rstd = sem("bn_rstd")
        s_bn_rstd_eps = sem("bn_rstd_eps")
        s_bn_var = sem("bn_var")
        s_back_scan = sem("back_scan")
        s_conv_ends = sem("conv_ends")
        s_back_carry = sem("back_carry")
        s_back_mask = [sem("back_mask_0"), sem("back_mask_1")]
        s_affine = sem("affine")
        s_conv_scan = sem("conv_scan")
        s_nb_ready = sem("nb_ready")
        s_nb_kept = sem("nb_kept")
        s_c_steps = sem("c_steps")
        s_c_turned = sem("c_turned")
        s_ids_turned = sem("ids_turned")
        s_hist_used = [sem("hist_used_0"), sem("hist_used_1")]
        s_hist_onehot = sem("hist_onehot")
        s_table_updated = [sem("table_updated_0"), sem("table_updated_1")]
        s_rank_onehot = sem("rank_onehot")
        s_looked_up = sem("looked_up")
        s_rank_parts = sem("rank_parts")
        s_scattered = [sem("scattered_0"), sem("scattered_1")]
        s_staged = sem("staged")
        s_gat_negmask = sem("gat_negmask")
        s_gat_normed = sem("gat_normed")
        s_gat_got = [sem("gat_got_0"), sem("gat_got_1")]
        s_gat_staged = sem("gat_staged")
        s_gat_turned = sem("gat_turned")
        s_gat_stat = sem("gat_stat")
        s_gat_mv = sem("gat_mv")
        s_gat_kept = sem("gat_kept")
        s_gat_score = sem("gat_score")
        s_gat_exp = sem("gat_exp")
        s_gat_den = sem("gat_den")
        s_gat_num = sem("gat_num")
        s_gat_args = sem("gat_args")
        s_gat_spread = sem("gat_spread")
        s_gat_nbias = sem("gat_nbias")
        s_gat_mask = [sem("gat_mask_0"), sem("gat_mask_1")]
        s_gat_logits = sem("gat_logits")
        s_gat_leak = sem("gat_leak")
        s_gat_max = sem("gat_max")
        s_gat_arg = sem("gat_arg")
        s_gat_den_rows = sem("gat_den_rows")
        s_gat_rows = sem("gat_rows")
        s_gat_stored = [sem("gat_stored_0"), sem("gat_stored_1")]
        s_gat_recip = sem("gat_recip")
        s_gat_bias = sem("gat_bias")
        s_gat_rstd = sem("gat_rstd")
        s_gat_rstd_eps = sem("gat_rstd_eps")
        s_conv_mask = [sem("conv_mask_0"), sem("conv_mask_1")]
        s_conv_got = [sem("conv_got_0"), sem("conv_got_1")]
        s_x1s_stored = [sem("x1s_stored_0"), sem("x1s_stored_1")]
        s_conv_turned = sem("conv_turned")
        s_conv_staged = sem("conv_staged")
        s_conv_kept = sem("conv_kept")
        s_conv_edge = sem("conv_edge")
        s_bn_steps = sem("bn_steps")
        s_flipped = sem("flipped")
        s_bn_ready = sem("bn_ready")
        s_nb_rows = sem("nb_rows")
        s_nb_stored = [sem("nb_stored_0"), sem("nb_stored_1")]
        s_x1s_ready = sem("x1s_ready")
        s_nb_got = [sem("nb_got_0"), sem("nb_got_1")]
        s_nb_staged = sem("nb_staged")
        s_dense_u = sem("dense_u")
        s_dense_x = [sem(f"dense_x_{b}") for b in range(RING)]
        s_dense_stat1 = sem("dense_stat1")
        s_dense_mv1 = sem("dense_mv1")
        s_dense_std = sem("dense_std")
        s_dense_newton = sem("dense_newton")
        s_dense_mean = sem("dense_mean")
        s_dense_y = sem("dense_y")
        s_dense_squares = sem("dense_squares")
        s_dense_shift2 = sem("dense_shift2")
        s_dense_normed = sem("dense_normed")
        s_dense_stored = [sem(f"dense_stored_{b}") for b in range(RING)]
        s_dense_done = sem("dense_done")
        s_fin_sum = sem("fin_sum")
        s_fidx_loaded = sem("fidx_loaded")
        s_fin_stat = sem("fin_stat")
        s_fin_mv = sem("fin_mv")
        s_fin_normed = sem("fin_normed")
        s_fin_done = [sem("fin_done_0"), sem("fin_done_1")]
        s_fin_staged = sem("fin_staged")
        s_fin_nbias = sem("fin_nbias")
        s_affine_last = sem("affine_last")
        s_fin_x = [sem("fin_x_0"), sem("fin_x_1")]
        s_fin_rstd = sem("fin_rstd")
        s_fin_rstd_eps = sem("fin_rstd_eps")
        s_go_pool = sem("go_pool")
        s_go_dve = sem("go_dve")
        s_go_act = sem("go_act")
        s_go_pe = sem("go_pe")
        s_go_sp = sem("go_sp")
        s_slot_staged = sem("slot_staged")
        s_slot_got = [sem("slot_got_0"), sem("slot_got_1")]
        s_gat_h = sem("gat_h")
        s_gat_msg = sem("gat_msg")
        s_conv_carry = sem("conv_carry")
        s_fin_rows = sem("fin_rows")
        s_conv_pad = sem("conv_pad")

        block = ctx.enter_context(nc.Block())

        def pairs(eng, body, count):
            body(0, 0, 0)
            body(1, 1, 0)
            n = (count - 3) // 2
            with eng.Fori(0, n) as i:
                body(2 * i + 2, 0, i + 1)
                body(2 * i + 3, 1, i + 1)
            for t in range(2 * n + 2, count):
                body(t, t % 2, t // 2)

        def lagged(eng, front, back, count):
            front(0, 0, 0)
            front(1, 1, 0)
            back(0, 0, 0)
            front(2, 0, 1)
            back(1, 1, 0)
            n = (count - 4) // 2
            with eng.Fori(0, n) as i:
                front(2 * i + 3, 1, i + 1)
                back(2 * i + 2, 0, i + 1)
                front(2 * i + 4, 0, i + 2)
                back(2 * i + 3, 1, i + 1)
            for t in range(2 * n + 3, count + 1):
                if t < count:
                    front(t, t % 2, t // 2)
                back(t - 1, (t - 1) % 2, (t - 1) // 2)


        def phased(eng, stages, count):
            first = max(lag for lag, _ in stages) + 2
            n = (count - first) // 2

            def step(s):
                for lag, f in stages:
                    if 0 <= s - lag < count:
                        f(s - lag, (s - lag) % 2, (s - lag) // 2)
            for s in range(first):
                step(s)
            with eng.Fori(0, n) as i:
                for s in (first, first + 1):
                    for lag, f in stages:
                        f(2 * i + s - lag, (s - lag) % 2, i + (s - lag) // 2)
            for s in range(first + 2 * n, count + first - 2):
                step(s)

        def setup_sync(sp):
            sp.wait_ge(s_pad_ids, 4)
            for k, ids in enumerate((dst, src)):
                sp.dma_start(krow[0:FULL, k, :], ids[0:FULL * P].rearrange("(c p) -> c p", p=P)).then_inc(s_ids, 16)
                sp.dma_start(krow[FULL:FULL + 1, k, 0:REST], ids[FULL * P:E].rearrange("(a p) -> a p", a=1)).then_inc(s_ids, 16)
                sp.dma_start(keyrow[k][:, 0:E], ids.partition_broadcast(P)).then_inc(s_ids, 16)
            for o, n in ((ord_dram[0], 2), (ord_dram[1], 4)):
                sp.dma_start(o[0:1, :], sentinel[0:1, 0:n]).then_inc(s_sentinels, 16)
                sp.dma_start(o[EP + 1:EP + 2, :], sentinel[1:2, 0:n]).then_inc(s_sentinels, 16)
            sp.dma_start(w_sb[:, :, :], w.rearrange("(k p) n -> p k n", p=P)).then_inc(s_params, 16)
            sp.dma_start(att[:, 0, :], att_src.partition_broadcast(P)).then_inc(s_params, 16)
            sp.dma_start(att[:, 1, :], att_dst.partition_broadcast(P)).then_inc(s_params, 16)
            sp.dma_start(bias_b[:, :], bias.partition_broadcast(P)).then_inc(s_params, 16)
            for l in range(L):
                sp.dma_start(thp[:, l, 0, :, :], theta_t[l].rearrange("(k p) n -> p k n", p=P)).then_inc(s_params, 16)
                sp.dma_start(thp[:, l, 1, :, :], phi_t[l].rearrange("(k p) n -> p k n", p=P)).then_inc(s_params, 16)
            with nc.allow_non_contiguous_dma(reason="small"):
                for t, a in enumerate((gammas, betas)):
                    sp.dma_start(gb[:, t, :, :], a).then_inc(s_params, 16)
        PARAMS = (4 + 2 * L + 2) * 16

        def setup_pool(pl):
            for k in range(2):
                pl.memset(keyrow[k][:, :], PADKEY).then_inc(s_pad_ids, 1)
            pl.memset(krow[:, :, :], PADKEY).then_inc(s_pad_ids, 1)
            pl.memset(sentinel[:, :], -1).then_inc(s_pad_ids, 1)
            pl.iota(iota_i[:, :], pattern=[[1, HI]], base=0, channel_multiplier=0).then_inc(s_pool_const, 1)
            pl.iota(iota_p[:, :], pattern=[[0, 1]], base=0, channel_multiplier=1,
                    allow_small_or_imprecise_dtypes=True).then_inc(s_pool_const, 1)
            for t, v in ((ident, 0.0), (below, 1.0), (above, 1.0), (head_rows, 1.0), (ones, 1.0), (neg_half, -0.5), (eps_b, EPS)):
                pl.memset(t[:, :], v).then_inc(s_pool_const, 1)
            pl.memset(zeros[:, :], 0.0).then_inc(s_pool_const, 1)
            pl.wait_ge(s_pool_const, 10)
            pl.affine_select(out=ident[:, :], in_=ident[:, :], compare_op=ALU.not_equal, fill=1.0, base=0,
                             pattern=[[-1, P]], channel_multiplier=1).then_inc(s_pool_const, 1)
            pl.affine_select(out=below[:, :], in_=below[:, :], compare_op=ALU.is_gt, fill=0.0, base=0,
                             pattern=[[-1, P]], channel_multiplier=1).then_inc(s_pool_const, 1)
            pl.affine_select(out=above[:, :], in_=above[:, :], compare_op=ALU.is_gt, fill=0.0, base=0,
                             pattern=[[1, P]], channel_multiplier=-1).then_inc(s_pool_const, 1)
            hr = head_rows[:, :].rearrange("p (a b) -> p a b", a=H)
            pl.affine_select(out=hr, in_=hr, compare_op=ALU.is_equal, fill=0.0, base=0,
                             pattern=[[-1, H], [0, HD]], channel_multiplier=1).then_inc(s_pool_const, 1)
        POOL_CONST = 14

        def setup_pe(pe):
            pe.wait_ge(s_pool_const, POOL_CONST)
            pe.wait_ge(s_ids_f, 1)
            for k in range(2):
                pe.transpose(bank[k][:, 0:NC], krow_f[:, k, :], ident[0:NC, 0:NC]).then_inc(s_ids_turned, 1)

        def setup_dve(v):
            v.wait_ge(s_ids, 6 * 16)
            v.tensor_copy(krow_f[:, :, :], krow[:, :, :]).then_inc(s_ids_f, 1)
            v.wait_ge(s_pool_const, POOL_CONST)
            n = 0

            def s(ins):
                nonlocal n
                n += 1
                ins.then_inc(s_setup, 1)
                v.wait_ge(s_setup, n)
            s(v.tensor_copy(iota_h[:, :], iota_i[:, :]))
            for k in range(2):
                v.wait_ge(s_ids_turned, k + 1)
                s(v.tensor_copy(key_f[:, k, :], bank[k][:, 0:NC]))
                s(v.tensor_copy(key_i[:, k, :], key_f[:, k, :]))
                s(v.tensor_scalar(lohi_i[:, k, 0, :], key_i[:, k, :], P - 1, None, ALU.bitwise_and))
                s(v.tensor_scalar(lohi_i[:, k, 1, :], key_i[:, k, :], 7, None, ALU.logical_shift_right))
                s(v.tensor_copy(lohi[:, k, :, :], lohi_i[:, k, :, :]))
                s(v.scalar_tensor_tensor(addr[:, k, :], lohi[:, k, 0, :], float(HI), lohi[:, k, 1, :], ALU.mult, ALU.add))
            s(v.tensor_copy(pay_d[:, :, 0], key_i[:, 1, :]))
            s(v.tensor_copy(pay_d[:, :, 1], key_i[:, 0, :]))
            v.wait_ge(s_params, PARAMS)
            s(v.tensor_scalar(rbias[:, :], bias_b[:, :], 0.0, None, ALU.max))
            for a in range(2):
                for k in range(2):
                    s(v.tensor_tensor(watt[:, k, :], w_sb[:, k, :], att[:, a, :], ALU.mult))
                    s(v.tensor_reduce(v_att[:, a, k, :], watt[:, k, :].rearrange("p (h d) -> p h d", h=H), AX.X, ALU.add))
            for l in range(L):
                s(v.tensor_tensor(thp[:, l, 1, :, :], thp[:, l, 1, :, :], thp[:, l, 0, :, :], ALU.subtract))
            v.sem_inc(s_weights_ready, 1)

        def onehot(v, k, par, c, s_ready):
            v.tensor_scalar(onelo[:, par, k, :], iota_h[:, 0:P], lohi[:, k, 0, bass.ds(c, 1)], None, ALU.is_equal).then_inc(s_ready, 1)
            v.tensor_scalar(onehi[:, par, k, :], iota_h[:, :], lohi[:, k, 1, bass.ds(c, 1)], None, ALU.is_equal).then_inc(s_ready, 1)

        def hist_dve(v):
            def body(c, par, u):
                v.wait_ge(s_hist_used[par], u)
                for k in range(2):
                    onehot(v, k, par, c, s_hist_onehot)
            pairs(v, body, NC)
            n = 0

            def s(ins):
                nonlocal n
                n += 1
                ins.then_inc(s_prefix, 1)
                v.wait_ge(s_prefix, n)
            v.wait_ge(s_hist_done, 1)
            for k in range(2):
                cnt = bank[k][:, 0:HI]
                s(v.tensor_tensor_scan(incl[:, k, :], ones[:, :], cnt, 0.0, ALU.mult, ALU.add))
            v.wait_ge(s_row_offsets, 1)
            s(v.tensor_copy(offs[:, :], bank[2][:, 0:2]))
            for k in range(2):
                cnt = bank[k][:, 0:HI]
                s(v.tensor_scalar(incl[:, k, :], incl[:, k, :], offs[:, k:k + 1], None, ALU.add))
                s(v.tensor_tensor(start[:, k, :], incl[:, k, :], cnt, ALU.subtract))
                s(v.tensor_scalar(junk[:, 0:HI], cnt, 0.0, float(NONE), ALU.is_equal, ALU.mult))
                s(v.scalar_tensor_tensor(slots[:, :, k], incl[:, k, :], 1.0, junk[:, 0:HI], ALU.subtract, ALU.add))

        def hist_pe(pe):
            pe.wait_ge(s_setup, 13)
            for k in range(2):
                pe.matmul(bank[k][:, 0:HI], zeros[:, 0:P], zeros[:, 0:HI], start=True, stop=False, skip_group_check=True)

            def body(c, par, u):
                pe.wait_ge(s_hist_onehot, 4 * c + 4)
                for k in range(2):
                    m = pe.matmul(bank[k][:, 0:HI], onelo[:, par, k, :], onehi[:, par, k, :], start=False, stop=False,
                                  skip_group_check=True)
                m.then_inc(s_hist_used[par], 1)
            pairs(pe, body, NC)
            for k in range(2):
                m = pe.matmul(bank[k][:, 0:HI], zeros[:, 0:P], zeros[:, 0:HI], start=False, stop=True, skip_group_check=True)
            m.then_inc(s_hist_done, 1)
            pe.wait_ge(s_prefix, 2)
            pe.matmul(bank[2][:, 0:2], above[:, :], incl[:, :, HI - 1], start=True, stop=True).then_inc(s_row_offsets, 1)

        def hist_sync(sp):
            sp.wait_ge(s_prefix, 11)
            sp.dma_start(table_dram.rearrange("(p r) c -> p r c", p=P), slots[:, :, :]).then_inc(s_table_stored, 16)

        def rank_dve(v, k):
            u0 = k * NC // 2
            c0 = k * NC
            def front(c, par, u):
                v.wait_ge(s_table_updated[par], u0 + u)
                if k or not is_first(c):
                    v.wait_ge(s_rank_parts, 2 * (c0 + c) - 2)
                v.tensor_scalar(lorow[:, :], keyrow[k][:, bass.ds(c * P, P)], P - 1, None, ALU.bitwise_and).then_inc(s_rank_onehot, 1)
                onehot(v, k, par, c, s_rank_onehot)
                v.wait_ge(s_rank_onehot, 4 * (c0 + c) + 1)
                v.tensor_scalar(lo_t[:, par, :], lorow[:, :], iota_p[:, 0:1], None, ALU.is_equal).then_inc(s_rank_onehot, 1)
                v.wait_ge(s_rank_onehot, 4 * (c0 + c) + 4)

            def back(c, par, u):
                v.wait_ge(s_looked_up, c0 + c + 1)
                v.scalar_tensor_tensor(junk[:, 0:HI], onehi[:, par, k, :], 1.0, bank[1 + par][:, 0:HI], ALU.mult, ALU.mult,
                                              accum_out=rank_a[:, k, bass.ds(c, 1)]).then_inc(s_rank_parts, 1)
                v.scalar_tensor_tensor(junk[:, HI:HI + P], keyrow[k][:, bass.ds(c * P, P)], key_f[:, k, bass.ds(c, 1)], below[:, :],
                                              ALU.is_equal, ALU.mult, accum_out=rank_b[:, k, bass.ds(c, 1)]).then_inc(s_rank_parts, 1)
                v.wait_ge(s_rank_parts, 2 * (c0 + c) + 2)
            lagged(v, front, back, NC)
            v.tensor_tensor(rank[:, k, :], rank_a[:, k, :], rank_b[:, k, :], ALU.add).then_inc(s_ranked, 1)
            v.wait_ge(s_ranked, 2 * k + 1)
            v.tensor_scalar(rank_i[:, k, :], rank[:, k, :], 1.0, None, ALU.add).then_inc(s_ranked, 1)
            v.wait_ge(s_ranked, 2 * k + 2)

        def rank_pe(pe, k):
            c0 = k * NC
            pe.wait_ge(s_prefix, 10)
            pe.wait_ge(s_table_copied, c0)
            pe.matmul(bank[0][:, 0:HI], ident[:, :], start[:, k, :], start=True, stop=False,
                      skip_group_check=True).then_inc(s_table_set, 1)

            def body(c, par, u):
                pe.wait_ge(s_rank_onehot, 4 * (c0 + c) + 4)
                pe.wait_ge(s_table_copied, c0 + c + 1)
                pe.matmul(bank[0][:, 0:HI], onelo[:, par, k, :], onehi[:, par, k, :], start=False, stop=False,
                          skip_group_check=True).then_inc(s_table_updated[par], 1)
                pe.matmul(bank[1 + par][:, 0:HI], lo_t[:, par, :], tab[:, par, :], start=True, stop=True).then_inc(s_looked_up, 1)
            pairs(pe, body, NC)

        def rank_act(a, k):
            u0 = k * NC // 2
            c0 = k * NC
            a.wait_ge(s_table_set, k + 1)

            def body(c, par, u):
                if par == 0:
                    a.wait_ge(s_table_updated[1], u0 + u)
                else:
                    a.wait_ge(s_table_updated[0], u0 + u + 1)
                a.activation(tab[:, par, :], bank[0][:, 0:HI], ACT.Copy).then_inc(s_table_copied, 1)
                a.wait_ge(s_table_copied, c0 + c + 1)
            pairs(a, body, NC)


        def scatter_pool(pl, k):
            width = (2, 4)[k]
            pay = (pay_d, pay_s)[k]
            pl.wait_ge(s_ranked, 2 * k + 2)
            pl.wait_ge(s_sentinels, 64)
            if k:
                pl.wait_ge(s_pay_s, 4)
            g0, u0 = k * NS, (k * (NS // 2 + 1), k * (NS // 2))

            def body(g, par, u):
                pl.wait_ge(s_scattered[par], 64 * (u + u0[par]))
                pl.sem_inc(s_go_pool, 1)
                pl.tensor_copy(st_i[:, par, :], rank_i[:, k, bass.ds(g * G, G)]).then_inc(s_staged, 1)
                pl.tensor_copy(st_pay[:, par, :, 0:width], pay[:, bass.ds(g * G, G), :]).then_inc(s_staged, 1)
                pl.wait_ge(s_staged, 2 * (g + g0) + 2)
                pl.sem_inc(s_go_pool, 1)
                for s in range(G):
                    pl.indirect_dma_start(ord_dram[k][:, :], bass.IndirectOffsetOnAxis(ap=st_i[:, par, s:s + 1], axis=0),
                                          st_pay[:, par, s, 0:width], None).then_inc(s_scattered[par], 16)
            pairs(pl, body, NS)
            pl.wait_ge(s_scattered[0], 64 * (u0[0] + NS // 2 + 1))
            pl.wait_ge(s_scattered[1], 64 * (u0[1] + NS // 2))
            pl.sem_inc(s_go_pool, 1)
            pl.sem_inc(s_order_ready, 1)


        def look_up_slots(pl):
            pl.wait_ge(s_table_stored, 16)
            for a in range(2):
                def body(g, par, u):
                    u = u + a * (NS // 2 + 1 - par)
                    g1 = g + a * NS
                    pl.wait_ge(s_slot_kept, g1)
                    pl.sem_inc(s_go_pool, 1)
                    pl.tensor_copy(st_i[:, par, :], addr[:, a, bass.ds(g * G, G)]).then_inc(s_slot_staged, 1)
                    pl.wait_ge(s_slot_staged, g1 + 1)
                    pl.sem_inc(s_go_pool, 1)
                    for s in range(G):
                        pl.indirect_dma_start(st_got[:, par, s, :], None, table_dram[:, :],
                                              bass.IndirectOffsetOnAxis(ap=st_i[:, par, s:s + 1], axis=0)).then_inc(s_slot_got[par], 16)
                    pl.wait_ge(s_slot_got[par], 64 * (u + 1))
                    pl.sem_inc(s_go_pool, 1)
                    pl.tensor_copy(found[:, bass.ds(g * G, G), a, :], st_got[:, par, :, :]).then_inc(s_slot_kept, 1)
                pairs(pl, body, NS)

        def payload_s(v):
            v.wait_ge(s_slot_kept, 2 * NS)
            v.wait_ge(s_ranked, 4)
            n = 0

            def s(ins):
                nonlocal n
                n += 1
                ins.then_inc(s_pay_s, 1)
                v.wait_ge(s_pay_s, n)
            v.tensor_copy(found_f[:, :, :, :], found[:, :, :, :]).then_inc(s_found_f, 1)
            v.wait_ge(s_found_f, 1)
            s(v.tensor_copy(pay_s[:, :, 0], key_i[:, 1, :]))
            s(v.scalar_tensor_tensor(pay_s[:, :, 1], rank[:, 0, :], float(EP), found_f[:, :, 1, 0], ALU.add, ALU.min))
            s(v.tensor_copy(pay_s[:, :, 2], found_f[:, :, 0, 0]))
            s(v.tensor_scalar(pay_s[:, :, 3], found_f[:, :, 0, 1], float(EP - 1), None, ALU.min))

        def order_sync(sp, k):
            o = ord_dram[k]
            w_ = (2, 4)[k]
            t = ordt if k == 0 else ords

            sp.wait_ge(s_order_ready, k + 1)
            kc = 1 - k
            if k == 0:
                sp.dma_start(ordt[:, 1:NC + 1, :], o[1:EP + 1, :].rearrange("(p r) c -> p r c", p=P)).then_inc(s_order[k], 16)
                sp.dma_start(ordt[:, 0:1, :], o[0:EP, :].rearrange("(p r) c -> p r c", p=P)[:, 0:1, :]).then_inc(s_order[k], 16)
                sp.dma_start(ordt[:, NC + 1:NC + 2, :], o[2:EP + 2, :].rearrange("(p r) c -> p r c", p=P)[:, NC - 1:NC, :]).then_inc(s_order[k], 16)
            else:
                sp.wait_ge(s_order_masks, 3)
                sp.dma_start(ords[:, :, :], o[1:EP + 1, :].rearrange("(p r) c -> p r c", p=P)).then_inc(s_order[k], 16)
                sp.dma_start(ordt[:, 0:1, :], o[0:EP, :].rearrange("(p r) c -> p r c", p=P)[:, 0:1, 0:2]).then_inc(s_order[k], 16)
                sp.dma_start(ordt[:, NC + 1:NC + 2, :], o[2:EP + 2, :].rearrange("(p r) c -> p r c", p=P)[:, NC - 1:NC, 0:2]).then_inc(s_order[k], 16)
            sp.wait_ge(s_order_masks, (3, 7)[k])
            sp.dma_start(same_dram[k][0:EP].rearrange("(p r) -> p r", p=P), cont[:, 0:NC]).then_inc(s_masks_stored, 16)
            sp.dma_start(same_dram[k][EP:EP + 1].rearrange("(a r) -> a r", a=1), cont[P - 1:P, NC:NC + 1]).then_inc(s_masks_stored, 16)
            sp.dma_start(fidx_dram[k].rearrange("(p r) -> p r", p=P), fin_i[:, :]).then_inc(s_masks_stored, 16)
            if k == 0:
                sp.dma_start(gidx_dram.rearrange("(p r) c -> p r c", p=P), gidx[:, :, :]).then_inc(s_masks_stored, 16)
            sp.wait_ge(s_masks_stored, (64, 112)[k])

        def order_dve(v, k):
            v.wait_ge(s_order[k], 48)
            n = 4 * k

            def s(ins):
                nonlocal n
                n += 1
                ins.then_inc(s_order_masks, 1)
                v.wait_ge(s_order_masks, n)
            if k == 0:
                s(v.tensor_scalar(gidx[:, :, :], ordt[:, 1:NC + 1, :], float(N - 1), None, ALU.min))
            else:
                v.wait_ge(s_masks_stored, 64)
                s(v.tensor_copy(ordt[:, 1:NC + 1, 0], ords[:, :, 0]))
            kc = 1 - k
            s(v.tensor_tensor(cont[:, :], ordt[:, 1:NC + 2, kc], ordt[:, 0:NC + 1, kc], ALU.is_equal))
            s(v.scalar_tensor_tensor(fin_i[:, :], cont[:, 1:NC + 1], float(SKIP), ordt[:, 1:NC + 1, kc], ALU.mult, ALU.add))
            if k == 0:
                v.sem_inc(s_order_masks, 1)
                v.wait_ge(s_order_masks, 4)

        rows_in = buf[:, 0:4096].rearrange("p (b a g f) -> p b a g f", b=2, a=2, g=G)
        rows_out = buf[:, 4096:8192].rearrange("p (b a g f) -> p b a g f", b=2, a=2, g=G)
        turned = buf[:, 8192:10240].rearrange("p (a j q) -> p a j q", a=2, j=2)
        wide = [hw, tpw]
        mask = sb("mask", [P, 2, SUP])
        mask_n = sb("mask_n", [P, 2, SUP])
        idx_all = sb("idx_all", [P, NS, G, 4], I32)
        idx_d = sb("idx_d", [P, NS, G, 2], I32)
        idx = sb("idx", [P, 2, G, 4], I32)
        stat = sb("stat", [P, 2 * DR, 6])
        mv = sb("mv", [P, 2 * DR, 2])
        rstd = sb("rstd", [P, 2, 2 * DR])
        nbias = sb("nbias", [P, 2, 2 * DR])
        tiny = sb("tiny", [P, G, H])
        rden = sb("rden", [P, G, H])

        def inv_std(pl, out_ap, var_ap, s_eps_added, s_done, eps_count):
            pl.tensor_scalar(out_ap, var_ap, EPS, None, ALU.add).then_inc(s_eps_added, 1)
            pl.wait_ge(s_eps_added, eps_count)
            pl.sem_inc(s_go_pool, 1)
            flat = out_ap.shape[1]
            pl.tensor_tensor(out_ap, out_ap, neg_half[0:out_ap.shape[0], 0:flat], ALU.pow).then_inc(s_done, 1)

        used = [0]

        def carve(n, rows=P):
            used[0] += n
            assert used[0] <= EP
            return big[0:rows, used[0] - n:used[0]]

        score = carve(SUP, H)
        negm = carve(SUP, H)
        runmax = [carve(SUP + 1, H) for _ in range(2)]
        args = carve(2 * SUP, H).rearrange("p (a q) -> p a q", a=2)
        expd = [carve(2 * SUP, H).rearrange("p (a q) -> p a q", a=2) for _ in range(2)]
        den = [carve(SUP, H) for _ in range(2)]
        h_sb = [carve(2 * SUP).rearrange("p (j q) -> p j q", j=2) for _ in range(2)]
        num = [carve(2 * SUP).rearrange("p (j q) -> p j q", j=2) for _ in range(2)]
        msg = carve(SUP)

        def by_slot(ap, s):
            return ap.rearrange("f (p g) -> f g p", g=G)[:, s, :]

        def turn_rows(pe, dst_bank, rows, j):
            for s in range(G):
                m = pe.transpose(dst_bank[:, s * P:(s + 1) * P], rows[:, s, j * P:(j + 1) * P], ident[:, :])
            return m

        def keep_turned(a, out_ap, bank_ap):
            return a.activation(out_ap.rearrange("f (p g) -> f g p", g=G), bank_ap.rearrange("f (g p) -> f g p", g=G), ACT.Copy)

        def norm_stats(v, s_stat, s_mv, rows, n, t):
            for r in range(n):
                v.bn_stats(stat[:rows[r].shape[0], r, :], rows[r]).then_inc(s_stat, 1)
            v.wait_ge(s_stat, n * t + n)
            v.sem_inc(s_go_dve, 1)
            for r in range(n):
                m = v.bn_aggr(mv[:rows[r].shape[0], r, :], stat[:rows[r].shape[0], r, :])
                m.then_inc(s_mv, 1)

        def gat_sync(sp):
            sp.wait_ge(s_masks_stored, 64)
            sp.dma_start(idx_d[:, :, :, :], gidx_dram.rearrange("(t p g) c -> p t g c", p=P, g=G)).then_inc(s_gat_idx, 16)

            def front(t, par, u):
                sp.wait_ge(s_gat_negmask, prev(t))
                sp.dma_start(mask[0:H, par, :], same_dram[0][bass.ds(t * SUP, SUP)].partition_broadcast(H)).then_inc(s_gat_mask[par], 16)

            def back(t, par, u):
                sp.wait_ge(s_gat_normed, 8 * (t + 1))
                for a in range(2):
                    sp.dma_start(x1_dram[bass.ds(a * EP + t * SUP, SUP), :].rearrange("(p g) f -> p g f", g=G),
                                 rows_out[:, par, a, :, :]).then_inc(s_gat_stored[par], 16)
            phased(sp, [(0, front), (2, back)], NS)
            sp.wait_ge(s_gat_stored[0], 32 * (NS // 2 + 1))
            sp.wait_ge(s_gat_stored[1], 32 * (NS // 2))
            sp.sem_inc(s_x1_ready, 1)

        def gat_pool(pl):
            pl.wait_ge(s_gat_idx, 16)
            pl.wait_ge(s_table_updated[0], NC)
            pl.wait_ge(s_table_updated[1], NC)
            pl.wait_ge(s_table_copied, 2 * NC)
            pl.wait_ge(s_pay_s, 4)

            def front(t, par, u):
                pl.wait_ge(s_gat_got[par], 128 * u)
                pl.wait_ge(s_gat_sums, 2 * prev(t))
                pl.sem_inc(s_go_pool, 1)
                pl.tensor_copy(idx[:, par, :, 0:2], idx_d[:, bass.ds(t, 1), :, :].rearrange("p a g c -> p (a g) c")).then_inc(s_gat_staged, 1)
                pl.wait_ge(s_gat_staged, t + 1)
                pl.wait_ge(s_gat_turned, 4 * prev(t))
                pl.sem_inc(s_go_pool, 1)
                for a in range(2):
                    for s in range(G):
                        pl.indirect_dma_start(rows_in[:, par, a, s, :], None, x[:, :],
                                              bass.IndirectOffsetOnAxis(ap=idx[:, par, s, a:a + 1], axis=0)).then_inc(s_gat_got[par], 16)

            def back(t, par, u):
                pl.wait_ge(s_gat_mv, 8 * (t + 1))
                pl.wait_ge(s_gat_normed, 8 * prev(t))
                pl.sem_inc(s_go_pool, 1)
                inv_std(pl, rstd[:, par, 0:8], mv[:, 0:8, 1], s_gat_rstd_eps, s_gat_rstd, t + 1)
            lagged(pl, front, back, NS)

        def gat_pe(pe):
            pe.wait_ge(s_weights_ready, 1)
            banks = wide[1]

            def front(t, par, u):
                pe.wait_ge(s_gat_got[par], 128 * (u + 1))
                if not is_first(t):
                    pe.wait_ge(s_gat_out, t)
                for n in range(4):
                    a, j = n // 2, n % 2
                    if n >= 2:
                        pe.wait_ge(s_gat_kept, 4 * t + n - 1)
                    turn_rows(pe, banks[:, j, :], rows_in[:, par, a, :, :], j).then_inc(s_gat_turned, 1)
                pe.wait_ge(s_gat_kept, 4 * t + 4)
                pe.wait_ge(s_gat_score, t)
                for n in range(4):
                    a, k = n // 2, n % 2
                    m = pe.matmul(bank[2][0:H, :], v_att[:, a, k, :], turned[:, a, k, :], start=(n == 0), stop=(n == 3))
                m.then_inc(s_gat_logits, 1)
                pe.wait_ge(s_gat_h_kept, 2 * t)
                for j in range(2):
                    for k in range(2):
                        m = pe.matmul(wide[0][:, j, :], w_sb[:, k, j * P:(j + 1) * P], turned[:, 0, k, :], start=(k == 0), stop=(k == 1))
                    m.then_inc(s_gat_h, 1)

            def back(t, par, u):
                pe.wait_ge(s_gat_exp, t + 1)
                for j in range(2):
                    pe.wait_ge(s_gat_num, 2 * t + j)
                    pe.matmul(bank[4][:, :], head_rows[:, j * P:(j + 1) * P], expd[par][:, 1, :], start=True, stop=True)
                    pe.matmul(bank[5][:, :], head_rows[:, j * P:(j + 1) * P], expd[par][:, 0, :], start=True, stop=True).then_inc(s_gat_spread, 1)
                pe.wait_ge(s_gat_den, t + 1)
                pe.wait_ge(s_gat_rden, t)
                pe.sem_inc(s_go_pe, 1)
                for s in range(G):
                    m = pe.transpose(bank[3][:, s * H:(s + 1) * H], by_slot(den[par], s), ident[0:H, 0:H])
                m.then_inc(s_gat_den_rows, 1)
                pe.wait_ge(s_gat_num, 2 * t + 2)
                for s in range(G):
                    for j in range(2):
                        m = pe.transpose(banks[:, s // 2, (s % 2) * D + j * P:(s % 2) * D + (j + 1) * P], by_slot(num[par][:, j, :], s), ident[:, :])
                m.then_inc(s_gat_rows, 1)
            phased(pe, [(1, back), (0, front)], NS)

        def gat_act(act):
            def front(t, par, u):
                for n in range(4):
                    a, j = n // 2, n % 2
                    if n == 0:
                        act.wait_ge(s_gat_h, 2 * t)
                    act.wait_ge(s_gat_turned, 4 * t + n + 1)
                    keep_turned(act, turned[:, a, j, :], wide[1][:, j, :]).then_inc(s_gat_kept, 1)
                act.wait_ge(s_gat_num, 2 * prev(t))
                for j in range(2):
                    act.wait_ge(s_gat_h, 2 * t + j + 1)
                    act.activation(h_sb[par][:, j, :], wide[0][:, j, :], ACT.Copy).then_inc(s_gat_h_kept, 1)
                act.wait_ge(s_gat_args, t + 1)
                act.wait_ge(s_gat_spread, 2 * prev(t))
                act.wait_ge(s_gat_den, prev(t))
                act.activation(expd[par][:, :, :], args[:, :, :], ACT.Exp).then_inc(s_gat_exp, 1)

            def back(t, par, u):
                act.wait_ge(s_gat_nbias, t + 1)
                for n in range(8):
                    o = rows_out[:, par, n // G, n % G, :]
                    act.activation(o, o, ACT.Identity, scale=rstd[:, par, n:n + 1], bias=nbias[:, par, n:n + 1]).then_inc(s_gat_normed, 1)
            phased(act, [(0, front), (2, back)], NS)

        def gat_dve(v):
            def front(t, par, u):
                v.wait_ge(s_gat_mask[par], 16 * (u + 1))
                v.tensor_scalar(negm, mask[0:H, par, :], BIG, -BIG, ALU.mult, ALU.add).then_inc(s_gat_negmask, 1)
                v.wait_ge(s_gat_negmask, t + 1)
                v.wait_ge(s_gat_logits, t + 1)
                v.tensor_scalar(score, bank[2][0:H, :], SLOPE, None, ALU.mult).then_inc(s_gat_leak, 1)
                v.wait_ge(s_gat_leak, t + 1)
                v.tensor_tensor(score, score, bank[2][0:H, :], ALU.max).then_inc(s_gat_score, 1)
                v.wait_ge(s_gat_score, t + 1)
                if is_first(t):
                    v.memset(runmax[0][:, 0:1], 0.0).then_inc(s_gat_max, 1)
                    v.wait_ge(s_gat_max, 1)
                else:
                    v.tensor_copy(runmax[par][:, 0:1], runmax[1 - par][:, SUP:SUP + 1]).then_inc(s_gat_max, 1)
                    v.wait_ge(s_gat_max, 2 * t + 1)
                v.tensor_tensor_scan(runmax[par][:, 1:SUP + 1], negm, score, runmax[par][:, 0:1], ALU.add, ALU.max).then_inc(s_gat_max, 1)
                v.wait_ge(s_gat_max, 2 * t + 2)
                v.wait_ge(s_gat_exp, t)
                v.tensor_tensor(args[:, 0, :], runmax[par][:, 0:SUP], negm, ALU.add).then_inc(s_gat_arg, 1)
                v.wait_ge(s_gat_arg, 2 * t + 1)
                v.tensor_tensor(args[:, 0, :], args[:, 0, :], runmax[par][:, 1:SUP + 1], ALU.subtract).then_inc(s_gat_arg, 1)
                v.wait_ge(s_gat_arg, 2 * t + 2)
                v.tensor_tensor(args[:, 1, :], score, runmax[par][:, 1:SUP + 1], ALU.subtract).then_inc(s_gat_args, 1)
                v.wait_ge(s_gat_args, t + 1)

            def back(t, par, u):
                first = is_first(t)
                v.wait_ge(s_gat_exp, t + 1)
                v.wait_ge(s_gat_den_rows, prev(t))
                v.tensor_tensor_scan(den[par], expd[par][:, 0, :], expd[par][:, 1, :],
                                            0.0 if first else den[1 - par][:, SUP - 1:SUP], ALU.mult, ALU.add).then_inc(s_gat_den, 1)
                v.wait_ge(s_gat_den, t + 1)
                v.wait_ge(s_gat_rows, prev(t))
                for j in range(2):
                    v.wait_ge(s_gat_h_kept, 2 * t + j + 1)
                    v.wait_ge(s_gat_spread, 2 * t + j + 1)
                    v.tensor_tensor(msg, h_sb[par][:, j, :], bank[4][:, :], ALU.mult).then_inc(s_gat_msg, 1)
                    v.wait_ge(s_gat_msg, 2 * t + j + 1)
                    v.tensor_tensor_scan(num[par][:, j, :], bank[5][:, :], msg,
                                                0.0 if first else num[1 - par][:, j, SUP - 1:SUP], ALU.mult, ALU.add).then_inc(s_gat_num, 1)
                    v.wait_ge(s_gat_num, 2 * t + j + 1)
                ya, yb = rows_out[:, par, 0, :, :], rows_out[:, par, 1, :, :]
                v.wait_ge(s_gat_stored[par], 32 * u)
                v.tensor_tensor(yb, rows_in[:, par, 0, :, :], rbias[:, :].unsqueeze(1).to_broadcast([P, G, D]), ALU.add).then_inc(s_gat_sums, 1)
                v.wait_ge(s_gat_sums, 2 * t + 1)
                v.wait_ge(s_gat_den_rows, t + 1)
                v.tensor_scalar(tiny[:, :, :], bank[3][:, 0:G * H].rearrange("p (g h) -> p g h", g=G), 1e-16, None, ALU.add).then_inc(s_gat_rden, 1)
                v.wait_ge(s_gat_rden, t + 1)
                v.reciprocal(rden[:, :, :], tiny[:, :, :]).then_inc(s_gat_recip, 1)
                v.wait_ge(s_gat_recip, t + 1)
                v.wait_ge(s_gat_rows, t + 1)
                v.tensor_tensor(ya.rearrange("p g (h d) -> p (g h) d", h=H), wide[1][:, :, :].rearrange("p b (h d) -> p (b h) d", d=HD),
                                       rden[:, :, :].rearrange("p g h -> p (g h)").unsqueeze(2).to_broadcast([P, G * H, HD]), ALU.mult).then_inc(s_gat_out, 1)
                v.wait_ge(s_gat_out, t + 1)
                v.tensor_tensor(ya, ya, bias_b[:, :].unsqueeze(1).to_broadcast([P, G, D]), ALU.add).then_inc(s_gat_bias, 1)
                v.wait_ge(s_gat_bias, t + 1)
                v.scalar_tensor_tensor(ya, ya, 0.0, rows_in[:, par, 1, :, :], ALU.max, ALU.add).then_inc(s_gat_sums, 1)
                v.wait_ge(s_gat_sums, 2 * t + 2)
                norm_stats(v, s_gat_stat, s_gat_mv, [rows_out[:, par, n // G, n % G, :] for n in range(8)], 8, t)

            def shift(t, par, u):
                v.wait_ge(s_gat_rstd, t + 1)
                v.wait_ge(s_gat_mv, 8 * (t + 1))
                v.scalar_tensor_tensor(nbias[:, par, 0:8], mv[:, 0:8, 0], -1.0, rstd[:, par, 0:8], ALU.mult, ALU.mult).then_inc(s_gat_nbias, 1)
                v.wait_ge(s_gat_nbias, t + 1)
            phased(v, [(2, shift), (1, back), (0, front)], NS)

        part = sb("part", [P, 2, 2, NS])
        tot = sb("tot", [P, 2, 2])
        bn = sb("bn", [P, 4, 2])
        bn_scale = sb("bn_scale", [P, 2])
        bn_shift = sb("bn_shift", [P, 2])
        ends = sb("ends", [P, 2, SUP])
        flipped = sb("flipped", [P, 2, 2, SUP])
        back_carry = sb("back_carry", [P, 2])
        c_rows = sb("c_rows", [P, D])
        sq = sb("sq", [P, SUP])

        def half(j, t):
            return state[:, j, bass.ds(t * SUP, SUP)]

        def conv_loads(sp, l):
            def load(t, par, u):
                tl = t + l * NS
                sp.wait_ge(s_conv_ends, 2 * (l * NS + prev(t)))
                sp.dma_start(mask[:, par, :], same_dram[1][bass.ds(t * SUP, SUP)].partition_broadcast(P)).then_inc(s_conv_mask[par], 16)
                sp.dma_start(mask_n[:, par, :], same_dram[1][bass.ds(t * SUP + 1, SUP)].partition_broadcast(P)).then_inc(s_conv_mask[par], 16)
            return load

        def conv_max(v, l):
            def body(t, par, u):
                tl = t + l * NS
                first, last = is_first(t), isinstance(t, int) and t == NS - 1
                v.wait_ge(s_conv_mask[par], 32 * (u + uses(l, par) + 1))
                for j in range(2):
                    v.wait_ge(s_conv_edge, 2 * tl + 2)
                    v.tensor_tensor_scan(half(j, t), mask[:, par, :], wide[par][:, j, :], state_carry[:, j:j + 1], ALU.mult, ALU.max).then_inc(s_conv_scan, 1)
                    v.wait_ge(s_conv_scan, 2 * tl + j + 1)
                    v.tensor_scalar(state_carry[:, j:j + 1], state[:, j, bass.ds(t * SUP + SUP - 1, 1)], 1.0, None, ALU.mult).then_inc(s_conv_carry, 1)
                    v.wait_ge(s_conv_carry, 2 * tl + j + 1)
                    if last:
                        v.memset(state[:, j, E:EP], 0.0).then_inc(s_conv_pad, 1)
                        v.wait_ge(s_conv_pad, 2 * l + j + 1)
                    if l or not is_first(t):
                        v.wait_ge(s_conv_squared, 2 * tl + j - 1)
                    v.sem_inc(s_go_dve, 1)
                    v.scalar_tensor_tensor(ends[:, j, :], mask_n[:, par, :], 0.0, half(j, t), ALU.is_equal, ALU.mult,
                                                  accum_out=part[:, 0, j, bass.ds(t, 1)]).then_inc(s_conv_ends, 1)
                    v.wait_ge(s_conv_ends, 2 * tl + j + 1)
            return body

        def conv_squares(a, l):
            def body(t, par, u):
                tl = t + l * NS
                for j in range(2):
                    a.wait_ge(s_conv_ends, 2 * tl + j + 1)
                    a.sem_inc(s_go_act, 1)
                    a.activation(sq[:, :], ends[:, j, :], ACT.Square, accum_out=part[:, 1, j, bass.ds(t, 1)]).then_inc(s_conv_squared, 1)
                    a.wait_ge(s_conv_squared, 2 * tl + j + 1)
            return body
        state_carry = sb("state_carry", [P, 2])

        def first_sync(sp):
            sp.wait_ge(s_masks_stored, 112)
            sp.dma_start(idx_all[:, :, :, :], ord_dram[1][1:EP + 1, :].rearrange("(t p g) c -> p t g c", p=P, g=G)).then_inc(s_conv_idx, 16)
            load = conv_loads(sp, 0)

            def back(t, par, u):
                sp.wait_ge(s_conv_got[par], 128 * (u + 1))
                sp.dma_start(x1s_dram[bass.ds(t * SUP, SUP), :].rearrange("(p g) f -> p g f", g=G), rows_in[:, par, 0, :, :]).then_inc(s_x1s_stored[par], 16)
            lagged(sp, load, back, NS)
            sp.wait_ge(s_x1s_stored[0], 16 * (NS // 2 + 1))
            sp.wait_ge(s_x1s_stored[1], 16 * (NS // 2))
            sp.sem_inc(s_x1s_ready, 1)

        def first_pool(pl):
            pl.wait_ge(s_conv_idx, 16)
            pl.wait_ge(s_x1_ready, 1)
            pl.wait_ge(s_gat_got[0], 128 * (NS // 2 + 1))
            pl.wait_ge(s_gat_got[1], 128 * (NS // 2))
            pl.wait_ge(s_gat_sums, 2 * NS)

            def body(t, par, u):
                pl.wait_ge(s_conv_got[par], 128 * u)
                pl.wait_ge(s_x1s_stored[par], 16 * u)
                pl.wait_ge(s_conv_turned, 4 * prev(t))
                pl.sem_inc(s_go_pool, 1)
                pl.tensor_copy(idx[:, par, :, :], idx_all[:, bass.ds(t, 1), :, :].rearrange("p a g c -> p (a g) c")).then_inc(s_conv_staged, 1)
                pl.wait_ge(s_conv_staged, t + 1)
                pl.sem_inc(s_go_pool, 1)
                for a in range(2):
                    for s in range(G):
                        pl.indirect_dma_start(rows_in[:, par, a, s, :], None, x1_dram[:, :],
                                              bass.IndirectOffsetOnAxis(ap=idx[:, par, s, a + 1:a + 2], axis=0)).then_inc(s_conv_got[par], 16)
            pairs(pl, body, NS)

        def first_pe(pe):
            pe.wait_ge(s_gat_rden, NS)
            pe.wait_ge(s_gat_out, NS)
            pe.wait_ge(s_gat_h_kept, 2 * NS)

            def body(t, par, u):
                pe.wait_ge(s_conv_got[par], 128 * (u + 1))
                pe.wait_ge(s_conv_kept, 4 * t)
                for n in range(4):
                    turn_rows(pe, bank[2 + n][:, :], rows_in[:, par, n // 2, :, :], n % 2).then_inc(s_conv_turned, 1)
                pe.wait_ge(s_conv_kept, 4 * t + 4)
                pe.wait_ge(s_conv_scan, 2 * prev(t))
                for j in range(2):
                    for n in range(4):
                        a, k = n // 2, n % 2
                        m = pe.matmul(wide[par][:, j, :], thp[:, 0, 1 - a, k, j * P:(j + 1) * P], turned[:, a, k, :], start=(n == 0), stop=(n == 3))
                    m.then_inc(s_conv_edge, 1)
            pairs(pe, body, NS)

        def first_act(a):
            square = conv_squares(a, 0)

            def front(t, par, u):
                a.wait_ge(s_conv_edge, 2 * t)
                for n in range(4):
                    a.wait_ge(s_conv_turned, 4 * t + n + 1)
                    keep_turned(a, turned[:, n // 2, n % 2, :], bank[2 + n][:, :]).then_inc(s_conv_kept, 1)
            lagged(a, front, square, NS)

        def first_dve(v):
            v.memset(state_carry[:, :], 0.0).then_inc(s_carry_zero, 1)
            v.wait_ge(s_carry_zero, 1)
            pairs(v, conv_max(v, 0), NS)

        def norm_dve(v, l):
            v.wait_ge(s_conv_squared, 2 * NS * (l + 1))
            n = 7 * l

            def s(ins):
                nonlocal n
                n += 1
                ins.then_inc(s_bn_steps, 1)
                v.wait_ge(s_bn_steps, n)
            s(v.tensor_reduce(tot[:, :, :], part[:, :, :, :], AX.X, ALU.add))
            s(v.tensor_scalar(bn[:, 0:2, :], tot[:, :, :], 1.0 / N, None, ALU.mult))
            s(v.tensor_tensor(bn[:, 2, :], bn[:, 0, :], bn[:, 0, :], ALU.mult))
            s(v.tensor_tensor(bn[:, 2, :], bn[:, 1, :], bn[:, 2, :], ALU.subtract))
            v.sem_inc(s_bn_var, 1)
            v.wait_ge(s_bn_rstd, l + 1)
            s(v.tensor_tensor(bn_scale[:, :], bn[:, 3, :], gb[:, 0, l, :], ALU.mult))
            s(v.tensor_tensor(bn[:, 2, :], bn[:, 0, :], bn_scale[:, :], ALU.mult))
            s(v.tensor_tensor(bn_shift[:, :], gb[:, 1, l, :], bn[:, 2, :], ALU.subtract))
            v.sem_inc(s_bn_ready, 1)

        def norm_pool(pl, l):
            pl.wait_ge(s_bn_var, l + 1)
            inv_std(pl, bn[:, 3, :], bn[:, 2, :], s_bn_rstd_eps, s_bn_rstd, l + 1)


        def back_load(sp, l, t, par, u):
            tl = l * NS + t
            sp.wait_ge(s_back_scan, 2 * (l * NS + prev(t)))
            sp.wait_ge(s_conv_ends, 2 * NS * (l + 1))
            sp.sem_inc(s_go_sp, 1)
            sp.dma_start(mask[:, par, :], same_dram[1][bass.ds((NS - 1 - t) * SUP + 1, SUP)].partition_broadcast(P)).then_inc(s_back_mask[par], 16)

        def flip(a, l, t, par, u):
            tl = l * NS + t
            a.wait_ge(s_back_carry, 2 * (l * NS + prev(t)))
            a.sem_inc(s_go_act, 1)
            for j in range(2):
                a.activation(flipped[:, par, j, ::-1], half(j, NS - 1 - t), ACT.Copy).then_inc(s_flipped, 1)

        def spread(v, l, t, par, u):
            tl = l * NS + t
            first = is_first(t)
            v.wait_ge(s_back_mask[par], 16 * (u + uses(l, par) + 1))
            for j in range(2):
                v.wait_ge(s_flipped, 2 * tl + j + 1)
                v.tensor_tensor_scan(flipped[:, par, j, :], mask[:, par, ::-1], flipped[:, par, j, :],
                                            0.0 if first else back_carry[:, j:j + 1], ALU.mult, ALU.max).then_inc(s_back_scan, 1)
                v.wait_ge(s_back_scan, 2 * tl + j + 1)
                v.tensor_copy(back_carry[:, j:j + 1], flipped[:, par, j, SUP - 1:SUP]).then_inc(s_back_carry, 1)
                v.wait_ge(s_back_carry, 2 * tl + j + 1)

        def affine(a, l, t, par, u, keep):
            tl = l * NS + t
            for j in range(2):
                a.wait_ge(s_back_scan, 2 * tl + j + 1)
                a.wait_ge(s_bn_ready, l + 1)
                a.sem_inc(s_go_act, 1)
                outs = [turned[:, par, j, :]] + ([half(j, NS - 1 - t)] if keep else [])
                for o in outs:
                    a.activation(o, flipped[:, par, j, ::-1], ACT.Relu, scale=bn_scale[:, j:j + 1],
                                 bias=bn_shift[:, j:j + 1]).then_inc(s_affine if keep else s_affine_last, 1)

        def neighbour_sync(sp, l):
            t0 = (l - 1) * NS
            def back(t, par, u):
                sp.wait_ge(s_nb_kept, 2 * (t0 + t) + 2)
                sp.sem_inc(s_go_sp, 1)
                sp.dma_start(nb_dram[bass.ds((NS - 1 - t) * SUP, SUP), :].rearrange("(p g) f -> p g f", g=G),
                             rows_out[:, par, 0, :, :]).then_inc(s_nb_stored[par], 16)
            phased(sp, [(0, lambda t, par, u: back_load(sp, l - 1, t, par, u)), (2, back)], NS)
            sp.wait_ge(s_nb_stored[0], 16 * (uses(l - 1, 0) + NS // 2 + 1))
            sp.wait_ge(s_nb_stored[1], 16 * (uses(l - 1, 1) + NS // 2))
            sp.sem_inc(s_nb_ready, 1)

        def neighbour_dve(v, l):
            pairs(v, lambda t, par, u: spread(v, l - 1, t, par, u), NS)
            v.wait_ge(s_affine, 4 * NS * l)
            v.memset(state_carry[:, :], 0.0).then_inc(s_carry_zero, 1)
            v.wait_ge(s_carry_zero, l + 1)

        def neighbour_act(a, l):
            t0 = (l - 1) * NS
            def front(t, par, u):
                if is_first(t):
                    a.wait_ge(s_conv_edge, 2 * NS * l)
                a.wait_ge(s_affine, 4 * (t0 + prev(t)))
                a.sem_inc(s_go_act, 1)
                flip(a, l - 1, t, par, u)

            def values(t, par, u):
                a.wait_ge(s_nb_rows, t0 + prev(t))
                a.sem_inc(s_go_act, 1)
                affine(a, l - 1, t, par, u, True)

            def keep_rows(t, par, u):
                a.wait_ge(s_nb_stored[par], 16 * (u + uses(l - 1, par)))
                a.wait_ge(s_nb_rows, t0 + t + 1)
                a.sem_inc(s_go_act, 1)
                for b in range(2):
                    a.activation(rows_out[:, par, 0, 2 * b:2 * b + 2, :].rearrange("p g f -> p (g f)"), wide[par][:, b, :], ACT.Copy).then_inc(s_nb_kept, 1)
            phased(a, [(0, front), (1, values), (2, keep_rows)], NS)

        def neighbour_pe(pe, l):
            t0 = (l - 1) * NS
            pe.wait_ge(s_conv_scan, 2 * NS * l)

            def body(t, par, u):
                pe.wait_ge(s_affine, 4 * (t0 + t) + 4)
                pe.wait_ge(s_nb_kept, 2 * (t0 + prev(t)))
                for s in range(G):
                    for k in range(2):
                        m = pe.matmul(wide[par][:, s // 2, (s % 2) * D:(s % 2 + 1) * D], by_slot(turned[:, par, k, :], s), thp[:, l, 0, k, :],
                                      start=(k == 0), stop=(k == 1), skip_group_check=True)
                m.then_inc(s_nb_rows, 1)
            pairs(pe, body, NS)


        def edge_sync(sp, l):
            sp.wait_ge(s_back_scan, 2 * NS * l)
            pairs(sp, conv_loads(sp, l), NS)

        def edge_pool(pl, l):
            pl.wait_ge(s_nb_ready, l)
            if l == 1:
                pl.wait_ge(s_conv_got[0], 128 * (NS // 2 + 1))
                pl.wait_ge(s_conv_got[1], 128 * (NS // 2))
                pl.wait_ge(s_x1s_ready, 1)
                pl.wait_ge(s_conv_turned, 4 * NS)

            def body(t, par, u):
                tl = (l - 1) * NS + t
                pl.wait_ge(s_nb_got[par], 64 * (u + uses(l - 1, par)))
                pl.wait_ge(s_conv_edge, 2 * (l * NS + prev(t)))
                pl.sem_inc(s_go_pool, 1)
                pl.tensor_copy(idx[:, par, :, :], idx_all[:, bass.ds(t, 1), :, :].rearrange("p a g c -> p (a g) c")).then_inc(s_nb_staged, 1)
                pl.wait_ge(s_nb_staged, tl + 1)
                pl.sem_inc(s_go_pool, 1)
                for s in range(G):
                    pl.indirect_dma_start(rows_in[:, par, 0, s, :], None, nb_dram[:, :],
                                          bass.IndirectOffsetOnAxis(ap=idx[:, par, s, 3:4], axis=0)).then_inc(s_nb_got[par], 16)
            pairs(pl, body, NS)

        def edge_pe(pe, l):
            pe.wait_ge(s_nb_kept, 2 * NS * l)
            pe.wait_ge(s_affine, 4 * NS * l)

            def body(t, par, u):
                tl = l * NS + t
                pe.wait_ge(s_conv_scan, 2 * (l * NS + prev(t)))
                for j in range(2):
                    for k in range(2):
                        pe.matmul(wide[par][:, j, :], thp[:, l, 1, k, j * P:(j + 1) * P], half(k, t), start=(k == 0), stop=False, skip_group_check=True)
                    if j == 0:
                        pe.wait_ge(s_nb_got[par], 64 * (u + uses(l - 1, par) + 1))
                    for s in range(G):
                        m = pe.matmul(by_slot(wide[par][:, j, :], s), rows_in[:, par, 0, s, j * P:(j + 1) * P], ident[:, :],
                                      start=False, stop=(s == G - 1), skip_group_check=True)
                    m.then_inc(s_conv_edge, 1)
            pairs(pe, body, NS)

        def edge_act(a, l):
            pairs(a, conv_squares(a, l), NS)

        def edge_dve(v, l):
            pairs(v, conv_max(v, l), NS)



        cvec = sb("cvec", [P, 2])
        cmat = sb("cmat", [P, P])
        fidx = sb("fidx", [P, 2, NS, G], I32)
        last = L - 1

        def last_state_dve(v):
            v.tensor_scalar(cvec[:, :], bn_shift[:, :], 0.0, None, ALU.max).then_inc(s_c_steps, 1)
            v.wait_ge(s_c_steps, 1)
            for j in range(2):
                v.wait_ge(s_c_turned, j)
                v.tensor_scalar(cmat[:, :], ones[:, 0:P], cvec[:, j:j + 1], None, ALU.mult).then_inc(s_c_steps, 1)
                v.wait_ge(s_c_steps, 2 + j)
            v.wait_ge(s_c_turned, 2)
            v.tensor_copy(c_rows[:, :], bank[2][:, 0:D]).then_inc(s_c_steps, 1)
            v.wait_ge(s_c_steps, 4)
            v.tensor_reduce(cvec[:, 0:1], c_rows[:, :], AX.X, ALU.add).then_inc(s_c_steps, 1)
            v.wait_ge(s_c_steps, 5)
            v.tensor_scalar(cvec[:, 1:2], cvec[:, 0:1], -1.0 / D, None, ALU.mult).then_inc(s_c_steps, 1)
            v.wait_ge(s_c_steps, 6)
            v.tensor_scalar(c_rows[:, :], c_rows[:, :], cvec[:, 1:2], None, ALU.add).then_inc(s_c_steps, 1)
            v.wait_ge(s_c_steps, 7)

        def last_state_pe(pe):
            for j in range(2):
                pe.wait_ge(s_c_steps, 2 + j)
                pe.matmul(bank[2][:, j * P:(j + 1) * P], cmat[:, :], ident[:, :], start=True, stop=True).then_inc(s_c_turned, 1)

        x_tile = buf[:, 0:RING * DR * D].rearrange("p (b r f) -> p b r f", b=RING, r=DR)
        y_tile = buf[:, RING * DR * D:2 * RING * DR * D].rearrange("p (b r f) -> p b r f", b=RING, r=DR)
        unused = flipped[:, :, :, :].rearrange("p a b q -> p (a b q)")[:, 0:DR * D].rearrange("p (r f) -> p r f", r=DR)
        stat1 = sb("stat1", [P, RING, DR, 6])
        moments = sb("moments", [P, RING, 2, DR, 2])
        std12 = sb("std12", [P, RING, 2, DR])
        inv12 = sb("inv12", [P, RING, 2, DR])
        step12 = sb("step12", [P, RING, 2, DR])
        neg_mean = sb("neg_mean", [P, RING, DR])
        shift2 = sb("shift2", [P, RING, DR])
        ROOT = 16
        assert ROOT * ROOT == D
        BACK = 2

        def staged(eng, stages):
            first = max(lag for lag, _, _ in stages) + RING
            n = (DT - first) // RING

            def step(s):
                for lag, f, count in stages:
                    t = s - lag
                    if 0 <= t < count:
                        f(t, t % RING, t // RING)
            for s in range(first):
                step(s)
            with eng.Fori(0, n) as i:
                for s in range(first, first + RING):
                    for lag, f, count in stages:
                        t = s - lag
                        f(RING * i + t, t % RING, i + t // RING)
            for s in range(first + RING * n, max(lag + count for lag, _, count in stages)):
                step(s)

        def both_norms(t):
            if isinstance(t, int) and not BACK <= t < DT:
                parts = []
                if t <= DT:
                    _, p, r = tile_rows(t)
                    parts.append((p, slice(0, 1), r))
                if t >= BACK:
                    _, p, r = tile_rows(t - BACK)
                    parts.append((p, slice(1, 2), r))
                return parts
            return [(P, slice(0, 2), DR)]

        def reused(t):
            return not (isinstance(t, int) and t < RING)

        def tile_rows(t):
            if isinstance(t, int) and t == DT:
                return slice(DT * P * DR, N), TAIL, 1
            return bass.ds(t * P * DR, P * DR), P, DR

        def dense_sync(sp):
            sp.wait_ge(s_conv_squared, 2 * NS * L)
            for k in range(2):
                sp.dma_start(fidx[:, k, :, :], fidx_dram[k].rearrange("(t p g) -> p t g", p=P, g=G)).then_inc(s_fidx_loaded, 16)

            def load(t, b, u):
                rows, p, r = tile_rows(t)
                if reused(t):
                    sp.wait_ge(s_dense_y, t - RING + 1)
                sp.dma_start(x_tile[0:p, b, 0:r, :], x[rows, :].rearrange("(p r) f -> p r f", r=r)).then_inc(s_dense_x[b], 16)

            def store(t, b, u):
                rows, p, r = tile_rows(t)
                sp.wait_ge(s_dense_normed, t + 1)
                sp.dma_start(out[rows, :].rearrange("(p r) f -> p r f", r=r), y_tile[0:p, b, 0:r, :]).then_inc(s_dense_stored[b], 16)
            staged(sp, [(0, load, DT + 1), (5, store, DT + 1)])
            for b in range(RING):
                sp.wait_ge(s_dense_stored[b], 16 * (DT // RING + (b <= DT % RING)))
            sp.sem_inc(s_dense_done, 1)

        def dense_pool(pl):
            def body(t, b, u):
                rows, p, r = tile_rows(t)
                pl.wait_ge(s_dense_x[b], 16 * (u + 1))
                pl.sem_inc(s_go_pool, 1)
                pl.tensor_tensor(x_tile[0:p, b, 0:r, :], x_tile[0:p, b, 0:r, :],
                                 rbias[0:p, :].unsqueeze(1).to_broadcast([p, r, D]), ALU.add).then_inc(s_dense_u, 1)
            staged(pl, [(0, body, DT + 1)])

        def dense_act(a):
            def stds(t, b, u):
                if not (isinstance(t, int) and t > DT):
                    a.wait_ge(s_dense_mv1, t + 1)
                if not (isinstance(t, int) and t < BACK):
                    a.wait_ge(s_dense_squares, t - BACK + 1)
                for p, m, r in both_norms(t):
                    last_part = a.activation(std12[0:p, b, m, 0:r], moments[0:p, b, m, 0:r, 1], ACT.Sqrt, bias=eps_b[0:p, :])
                last_part.then_inc(s_dense_std, 1)

            def squares(t, b, u):
                rows, p, r = tile_rows(t)
                a.wait_ge(s_dense_y, t + 1)
                if not is_first(t):
                    a.wait_ge(s_dense_squares, t)
                for n in range(r):
                    m = a.activation(unused[0:p, n, :], y_tile[0:p, b, n, :], ACT.Square, scale=1.0 / ROOT, bias=neg_mean[0:p, b, n:n + 1],
                                     accum_out=moments[0:p, (b + BACK) % RING, 1, n, 1:2])
                m.then_inc(s_dense_squares, 1)

            def normed(t, b, u):
                rows, p, r = tile_rows(t)
                a.wait_ge(s_dense_shift2, t + 1)
                for n in range(r):
                    o = y_tile[0:p, b, n, :]
                    m = a.activation(o, o, ACT.Identity, scale=inv12[0:p, (b + BACK) % RING, 1, n:n + 1], bias=shift2[0:p, b, n:n + 1])
                m.then_inc(s_dense_normed, 1)
            staged(a, [(0, stds, DT + 1 + BACK), (BACK + 1, normed, DT + 1), (1, squares, DT + 1)])

        def dense_dve(v):
            def stats(t, b, u):
                rows, p, r = tile_rows(t)
                v.wait_ge(s_dense_u, t + 1)
                for n in range(r):
                    m = v.bn_stats(stat1[0:p, b, n, :], x_tile[0:p, b, n, :])
                m.then_inc(s_dense_stat1, 1)

            def means(t, b, u):
                rows, p, r = tile_rows(t)
                v.wait_ge(s_dense_stat1, t + 1)
                v.sem_inc(s_go_dve, 1)
                for n in range(r):
                    m = v.bn_aggr(moments[0:p, b, 0, n, :], stat1[0:p, b, n, :])
                m.then_inc(s_dense_mv1, 1)

            def reciprocals(t, b, u):
                v.wait_ge(s_dense_std, t + 1)
                v.sem_inc(s_go_dve, 1)
                for p, m, r in both_norms(t):
                    last_part = v.reciprocal(inv12[0:p, b, m, 0:r], std12[0:p, b, m, 0:r])
                last_part.then_inc(s_dense_newton, 1)
                v.wait_ge(s_dense_newton, 4 * t + 1)
                for p, m, r in both_norms(t):
                    i = inv12[0:p, b, m, 0:r]
                    last_part = v.scalar_tensor_tensor(step12[0:p, b, m, 0:r], i, -0.5, i, ALU.mult, ALU.mult)
                last_part.then_inc(s_dense_newton, 1)
                v.wait_ge(s_dense_newton, 4 * t + 2)
                for p, m, r in both_norms(t):
                    o = step12[0:p, b, m, 0:r]
                    last_part = v.scalar_tensor_tensor(o, moments[0:p, b, m, 0:r, 1], EPS, o, ALU.add, ALU.mult)
                last_part.then_inc(s_dense_newton, 1)
                v.wait_ge(s_dense_newton, 4 * t + 3)
                for p, m, r in both_norms(t):
                    i = inv12[0:p, b, m, 0:r]
                    last_part = v.scalar_tensor_tensor(i, step12[0:p, b, m, 0:r], 1.5, i, ALU.add, ALU.mult)
                last_part.then_inc(s_dense_newton, 1)

            def sums(t, b, u):
                rows, p, r = tile_rows(t)
                v.wait_ge(s_dense_newton, 4 * t + 4)
                v.scalar_tensor_tensor(neg_mean[0:p, b, 0:r], moments[0:p, b, 0, 0:r, 0], -1.0 / ROOT, inv12[0:p, b, 0, 0:r],
                                       ALU.mult, ALU.mult).then_inc(s_dense_mean, 1)
                if reused(t):
                    v.wait_ge(s_dense_stored[b], 16 * u)
                for n in range(r):
                    m = v.scalar_tensor_tensor(y_tile[0:p, b, n, :], x_tile[0:p, b, n, :], inv12[0:p, b, 0, n:n + 1], c_rows[0:p, :], ALU.mult, ALU.add)
                m.then_inc(s_dense_y, 1)

            def shift(t, b, u):
                rows, p, r = tile_rows(t)
                v.wait_ge(s_dense_newton, 4 * (t + BACK) + 4)
                v.wait_ge(s_dense_mean, t + 1)
                v.scalar_tensor_tensor(shift2[0:p, b, 0:r], neg_mean[0:p, b, 0:r], float(ROOT), inv12[0:p, (b + BACK) % RING, 1, 0:r],
                                       ALU.mult, ALU.mult).then_inc(s_dense_shift2, 1)
            staged(v, [(1, reciprocals, DT + 1 + BACK), (BACK + 1, shift, DT + 1), (1, sums, DT + 1), (0, stats, DT + 1), (0, means, DT + 1)])

        def final_sync(sp, kind):
            f0 = kind * NS
            if kind == 0:
                sp.wait_ge(s_dense_done, 1)

            def front(t, par, u):
                sp.wait_ge(s_fin_sum, f0 + prev(t))
                sp.sem_inc(s_go_sp, 1)
                r = t if kind == 0 else NS - 1 - t
                source = x1_dram if kind == 0 else x1s_dram
                sp.dma_start(rows_in[:, par, 0, :, :], source[bass.ds(r * SUP, SUP), :].rearrange("(p g) f -> p g f", g=G)).then_inc(s_fin_x[par], 16)

            def masks(t, par, u):
                back_load(sp, last, t, par, u)
            phased(sp, [(0, masks), (2, front)] if kind else [(0, front)], NS)
            if kind:
                sp.wait_ge(s_fin_done[0], 64 * (2 * (NS // 2) + 2))
                sp.wait_ge(s_fin_done[1], 64 * 2 * (NS // 2))

        def final_pool(pl, kind):
            f0 = kind * NS
            if kind == 0:
                pl.wait_ge(s_fidx_loaded, 32)
                pl.wait_ge(s_dense_done, 1)

            def front(t, par, u):
                tf = f0 + t
                pl.wait_ge(s_fin_mv, G * (tf + 1))
                pl.wait_ge(s_fin_normed, G * (f0 + prev(t)))
                pl.sem_inc(s_go_pool, 1)
                inv_std(pl, rstd[:, par, 0:G], mv[:, 0:G, 1], s_fin_rstd_eps, s_fin_rstd, tf + 1)
                r = t if kind == 0 else NS - 1 - t
                pl.wait_ge(s_fin_done[par], 64 * (u + uses(kind, par)))
                pl.sem_inc(s_go_pool, 1)
                pl.tensor_copy(idx[:, par, :, 0], fidx[:, kind, bass.ds(r, 1), :].rearrange("p a g -> p (a g)")).then_inc(s_fin_staged, 1)

            def back(t, par, u):
                tf = f0 + t
                pl.wait_ge(s_fin_normed, G * (tf + 1))
                pl.wait_ge(s_fin_staged, tf + 1)
                pl.sem_inc(s_go_pool, 1)
                for s in range(G):
                    pl.indirect_dma_start(out[:, :], bass.IndirectOffsetOnAxis(ap=idx[:, par, s, 0:1], axis=0), rows_out[:, par, 0, s, :], None,
                                          bounds_check=N - 1, oob_is_err=False).then_inc(s_fin_done[par], 16)
            lagged(pl, front, back, NS)
            pl.wait_ge(s_fin_done[0], 64 * (kind + 1) * (NS // 2 + 1))
            pl.wait_ge(s_fin_done[1], 64 * (kind + 1) * (NS // 2))

        def final_act(a, kind):
            f0 = kind * NS
            def turned_back(t, par, u):
                a.wait_ge(s_affine_last, 2 * prev(t))
                a.sem_inc(s_go_act, 1)
                flip(a, last, t, par, u)

            def state_values(t, par, u):
                a.wait_ge(s_fin_rows, prev(t))
                a.sem_inc(s_go_act, 1)
                affine(a, last, t, par, u, False)

            def normed(t, par, u):
                a.wait_ge(s_fin_nbias, f0 + t + 1)
                for n in range(G):
                    o = rows_out[:, par, 0, n, :]
                    a.activation(o, o, ACT.Identity, scale=rstd[:, par, n:n + 1], bias=nbias[:, par, n:n + 1]).then_inc(s_fin_normed, 1)
            phased(a, ([(0, turned_back), (1, state_values)] if kind else []) + [(3, normed)], NS)

        def final_pe(pe, kind):
            f0 = kind * NS
            def body(t, par, u):
                pe.wait_ge(s_affine_last, 2 * t + 2)
                pe.wait_ge(s_fin_sum, f0 + prev(t))
                for s in range(G):
                    for k in range(2):
                        m = pe.transpose(wide[par][:, s // 2, (s % 2) * D + k * P:(s % 2) * D + (k + 1) * P], by_slot(turned[:, par, k, :], s), ident[:, :])
                m.then_inc(s_fin_rows, 1)
            pairs(pe, body, NS)

        def final_dve(v, kind):
            f0 = kind * NS
            if kind == 0:
                v.wait_ge(s_dense_done, 1)

            def spread_back(t, par, u):
                spread(v, last, t, par, u)

            def sums(t, par, u):
                tf = f0 + t
                y = rows_out[:, par, 0, :, :]
                if kind:
                    v.wait_ge(s_fin_rows, t + 1)
                v.wait_ge(s_fin_x[par], 16 * (u + uses(kind, par) + 1))
                v.wait_ge(s_fin_done[par], 64 * (u + uses(kind, par)))
                other = wide[par][:, :, :].rearrange("p b (s f) -> p (b s) f", f=D) if kind else c_rows[:, :].unsqueeze(1).to_broadcast([P, G, D])
                v.tensor_tensor(y, other, rows_in[:, par, 0, :, :], ALU.add).then_inc(s_fin_sum, 1)
                v.wait_ge(s_fin_sum, tf + 1)
                norm_stats(v, s_fin_stat, s_fin_mv, [rows_out[:, par, 0, n, :] for n in range(G)], G, tf)

            def shift(t, par, u):
                tf = f0 + t
                v.wait_ge(s_fin_rstd, tf + 1)
                v.wait_ge(s_fin_mv, G * (tf + 1))
                v.scalar_tensor_tensor(nbias[:, par, 0:G], mv[:, 0:G, 0], -1.0, rstd[:, par, 0:G], ALU.mult, ALU.mult).then_inc(s_fin_nbias, 1)
                v.wait_ge(s_fin_nbias, tf + 1)
            phased(v, ([(0, spread_back)] if kind else []) + [(3, shift), (2, sums)], NS)

        @block.sync
        def _(sp):
            setup_sync(sp)
            hist_sync(sp)
            for k in range(2):
                order_sync(sp, k)
            gat_sync(sp)
            first_sync(sp)
            for l in range(1, L):
                neighbour_sync(sp, l)
                edge_sync(sp, l)
            dense_sync(sp)
            for kind in range(2):
                final_sync(sp, kind)

        @block.gpsimd
        def _(pool):
            setup_pool(pool)
            scatter_pool(pool, 0)
            look_up_slots(pool)
            scatter_pool(pool, 1)
            gat_pool(pool)
            first_pool(pool)
            norm_pool(pool, 0)
            for l in range(1, L):
                edge_pool(pool, l)
                norm_pool(pool, l)
            dense_pool(pool)
            for kind in range(2):
                final_pool(pool, kind)

        @block.scalar
        def _(act):
            for k in range(2):
                rank_act(act, k)
            gat_act(act)
            first_act(act)
            for l in range(1, L):
                neighbour_act(act, l)
                edge_act(act, l)
            dense_act(act)
            for kind in range(2):
                final_act(act, kind)

        @block.vector
        def _(dve):
            setup_dve(dve)
            hist_dve(dve)
            rank_dve(dve, 0)
            order_dve(dve, 0)
            rank_dve(dve, 1)
            payload_s(dve)
            order_dve(dve, 1)
            gat_dve(dve)
            first_dve(dve)
            norm_dve(dve, 0)
            for l in range(1, L):
                neighbour_dve(dve, l)
                edge_dve(dve, l)
                norm_dve(dve, l)
            last_state_dve(dve)
            dense_dve(dve)
            for kind in range(2):
                final_dve(dve, kind)

        @block.tensor
        def _(pe):
            setup_pe(pe)
            hist_pe(pe)
            for k in range(2):
                rank_pe(pe, k)
            gat_pe(pe)
            first_pe(pe)
            for l in range(1, L):
                neighbour_pe(pe, l)
                edge_pe(pe, l)
            last_state_pe(pe)
            final_pe(pe, 1)


def layout(x, src, dst, L0_gnn_W, L0_gnn_att_src, L0_gnn_att_dst, L0_gnn_bias,
           L1_gnn_thetas, L1_gnn_phis, L1_gnn_gammas, L1_gnn_betas):
    import numpy as np
    by_feature = lambda a: np.ascontiguousarray(np.asarray(a).reshape(L, 2, P).transpose(2, 0, 1))
    turned = lambda a: np.ascontiguousarray(np.asarray(a).transpose(0, 2, 1))
    return {
        "x": np.ascontiguousarray(x), "src": np.ascontiguousarray(src), "dst": np.ascontiguousarray(dst),
        "w": np.ascontiguousarray(L0_gnn_W).reshape(D, D), "att_src": np.ascontiguousarray(L0_gnn_att_src).reshape(D),
        "att_dst": np.ascontiguousarray(L0_gnn_att_dst).reshape(D), "bias": np.ascontiguousarray(L0_gnn_bias),
        "theta_t": turned(L1_gnn_thetas), "phi_t": turned(L1_gnn_phis),
        "gammas": by_feature(L1_gnn_gammas), "betas": by_feature(L1_gnn_betas),
    }


def kernel(x, src, dst, L0_gnn_W, L0_gnn_att_src, L0_gnn_att_dst, L0_gnn_bias,
           L1_gnn_thetas, L1_gnn_phis, L1_gnn_gammas, L1_gnn_betas):
    import numpy as np
    import concourse.bacc as bacc
    from concourse.bass_utils import run_bass_kernel_spmd

    nc = bacc.Bacc("TRN2", target_bir_lowering=False, num_devices=1)
    arrays = layout(x, src, dst, L0_gnn_W, L0_gnn_att_src, L0_gnn_att_dst, L0_gnn_bias,
                    L1_gnn_thetas, L1_gnn_phis, L1_gnn_gammas, L1_gnn_betas)
    args = [nc.dram_tensor(name, a.shape, mybir.dt.from_np(a.dtype), kind="ExternalInput").ap() for name, a in arrays.items()]
    out = nc.dram_tensor("out", (N, D), F32, kind="ExternalOutput").ap()
    gnn(nc, *args, out)
    run = run_bass_kernel_spmd(nc, [arrays], core_ids=[0])
    return run.results[0]["out"]
```
